# Optimizing a Trainium2 kernel written in Bass

```python
import numpy as np
import jax
import jax.numpy as jnp

def _softmax(x, axis=-1):
    return jax.nn.softmax(x, axis=axis)

def _gelu(x):
    return jax.nn.gelu(x, approximate=True)

def _silu(x):
    return jax.nn.silu(x)

def _sigmoid(x):
    return jax.nn.sigmoid(x)

def _layernorm(x, axis=-1, eps=1e-05):
    m = jnp.mean(x, axis=axis, keepdims=True)
    v = jnp.var(x, axis=axis, keepdims=True)
    return (x - m) / jnp.sqrt(v + eps)

def _scatter_add(tgt, idx, src, axis=0):
    return tgt.at[idx].add(src)

def _segment_sum(src, seg, n):
    return jax.ops.segment_sum(src, seg, n)
kernel_name = 'mk_rec_standalone_d1_rec_r8_22a765'

def setup_inputs(seed: int=0):
    np.random.seed(seed)
    _w = jnp.asarray

    def _rec_inputs():
        import jax
        import jax.numpy as jnp
        _rk = jax.random.key(seed)
        r_numeric_feats = -0.0032598 + 0.998017 * jax.random.normal(jax.random.fold_in(_rk, 1), (1024, 13), jnp.float32)
        r_user_input = jax.random.randint(jax.random.fold_in(_rk, 2), (1024,), 17, 99964, jnp.int32)
        r_item_input = jax.random.randint(jax.random.fold_in(_rk, 3), (1024,), 13, 99986, jnp.int32)
        r_categorical_feats = jnp.stack([jax.random.randint(jax.random.fold_in(jax.random.fold_in(_rk, 4), 0), (1024,), 0, 1250, jnp.int32), jax.random.randint(jax.random.fold_in(jax.random.fold_in(_rk, 4), 1), (1024,), 0, 9999, jnp.int32), jax.random.randint(jax.random.fold_in(jax.random.fold_in(_rk, 4), 2), (1024,), 0, 1250, jnp.int32), jax.random.randint(jax.random.fold_in(jax.random.fold_in(_rk, 4), 3), (1024,), 0, 1250, jnp.int32), jax.random.randint(jax.random.fold_in(jax.random.fold_in(_rk, 4), 4), (1024,), 0, 1250, jnp.int32), jax.random.randint(jax.random.fold_in(jax.random.fold_in(_rk, 4), 5), (1024,), 0, 1250, jnp.int32), jax.random.randint(jax.random.fold_in(jax.random.fold_in(_rk, 4), 6), (1024,), 1, 1250, jnp.int32), jax.random.randint(jax.random.fold_in(jax.random.fold_in(_rk, 4), 7), (1024,), 0, 1250, jnp.int32), jax.random.randint(jax.random.fold_in(jax.random.fold_in(_rk, 4), 8), (1024,), 0, 1250, jnp.int32), jax.random.randint(jax.random.fold_in(jax.random.fold_in(_rk, 4), 9), (1024,), 0, 9999, jnp.int32), jax.random.randint(jax.random.fold_in(jax.random.fold_in(_rk, 4), 10), (1024,), 0, 1250, jnp.int32), jax.random.randint(jax.random.fold_in(jax.random.fold_in(_rk, 4), 11), (1024,), 0, 1250, jnp.int32), jax.random.randint(jax.random.fold_in(jax.random.fold_in(_rk, 4), 12), (1024,), 2, 1250, jnp.int32), jax.random.randint(jax.random.fold_in(jax.random.fold_in(_rk, 4), 13), (1024,), 2, 1250, jnp.int32), jax.random.randint(jax.random.fold_in(jax.random.fold_in(_rk, 4), 14), (1024,), 0, 1250, jnp.int32), jax.random.randint(jax.random.fold_in(jax.random.fold_in(_rk, 4), 15), (1024,), 2, 1250, jnp.int32), jax.random.randint(jax.random.fold_in(jax.random.fold_in(_rk, 4), 16), (1024,), 0, 1250, jnp.int32), jax.random.randint(jax.random.fold_in(jax.random.fold_in(_rk, 4), 17), (1024,), 1, 1250, jnp.int32), jax.random.randint(jax.random.fold_in(jax.random.fold_in(_rk, 4), 18), (1024,), 1, 9999, jnp.int32), jax.random.randint(jax.random.fold_in(jax.random.fold_in(_rk, 4), 19), (1024,), 0, 1250, jnp.int32), jax.random.randint(jax.random.fold_in(jax.random.fold_in(_rk, 4), 20), (1024,), 0, 1250, jnp.int32), jax.random.randint(jax.random.fold_in(jax.random.fold_in(_rk, 4), 21), (1024,), 0, 1250, jnp.int32), jax.random.randint(jax.random.fold_in(jax.random.fold_in(_rk, 4), 22), (1024,), 0, 1250, jnp.int32), jax.random.randint(jax.random.fold_in(jax.random.fold_in(_rk, 4), 23), (1024,), 0, 1250, jnp.int32), jax.random.randint(jax.random.fold_in(jax.random.fold_in(_rk, 4), 24), (1024,), 0, 1250, jnp.int32), jax.random.randint(jax.random.fold_in(jax.random.fold_in(_rk, 4), 25), (1024,), 0, 1250, jnp.int32)], axis=1)
        return (r_numeric_feats, r_user_input, r_item_input, r_categorical_feats)
    r_numeric_feats, r_user_input, r_item_input, r_categorical_feats = _rec_inputs()

    def _L0_rec_setup():
        import jax, jax.numpy as jnp
        import numpy as np
        B = 2048
        EMB = 64
        N_NUM = 13
        N_CAT = 26
        CAT_VOCAB = 1250
        N_USERS = 12500
        N_ITEMS = 12500
        D = (2 + N_NUM + N_CAT) * EMB
        MLP_DIM = 1024
        N_MLP = 4
        L_CROSS = 4
        key = jax.random.key(seed)
        ks = jax.random.split(key, 20)
        s = 0.02
        return {'user_input': jax.random.randint(ks[0], (B,), 0, N_USERS), 'item_input': jax.random.randint(ks[1], (B,), 0, N_ITEMS), 'numeric_feats': jax.random.normal(ks[2], (B, N_NUM), jnp.float32), 'categorical_feats': jax.random.randint(ks[3], (B, N_CAT), 0, CAT_VOCAB), 'user_emb': jax.random.normal(ks[4], (N_USERS, EMB), jnp.float32) * s, 'item_emb': jax.random.normal(ks[5], (N_ITEMS, EMB), jnp.float32) * s, 'cat_tables': jax.random.normal(ks[6], (N_CAT, CAT_VOCAB, EMB), jnp.float32) * s, 'num_W': jax.random.normal(ks[7], (N_NUM, EMB), jnp.float32) * s, 'num_b': jax.random.normal(ks[8], (N_NUM, EMB), jnp.float32) * s, 'Wc': jax.random.normal(ks[9], (L_CROSS, D, D), jnp.float32) * s, 'bc': jax.random.normal(ks[10], (L_CROSS, D), jnp.float32) * s, 'W0': jax.random.normal(ks[11], (D, MLP_DIM), jnp.float32) * s, 'b0': jax.random.normal(ks[12], (MLP_DIM,), jnp.float32) * s, 'Wh': jax.random.normal(ks[13], (N_MLP - 1, MLP_DIM, MLP_DIM), jnp.float32) * s, 'bh': jax.random.normal(ks[14], (N_MLP - 1, MLP_DIM), jnp.float32) * s, 'Wf': jax.random.normal(ks[15], (D + MLP_DIM, 1), jnp.float32) * s, 'bf': jax.random.normal(ks[16], (1,), jnp.float32) * s}
    _L0_rec_all = _L0_rec_setup()
    _L0_rec_in = {k: v for k, v in _L0_rec_all.items() if k in ('user_emb', 'item_emb', 'cat_tables', 'num_W', 'num_b', 'Wc', 'bc', 'W0', 'b0', 'Wh', 'bh', 'Wf', 'bf')}
    del _L0_rec_all
    return {'r_numeric_feats': r_numeric_feats, 'r_user_input': r_user_input, 'r_item_input': r_item_input, 'r_categorical_feats': r_categorical_feats, 'L0_rec_user_emb': _L0_rec_in['user_emb'], 'L0_rec_item_emb': _L0_rec_in['item_emb'], 'L0_rec_cat_tables': _L0_rec_in['cat_tables'], 'L0_rec_num_W': _L0_rec_in['num_W'], 'L0_rec_num_b': _L0_rec_in['num_b'], 'L0_rec_Wc': _L0_rec_in['Wc'], 'L0_rec_bc': _L0_rec_in['bc'], 'L0_rec_W0': _L0_rec_in['W0'], 'L0_rec_b0': _L0_rec_in['b0'], 'L0_rec_Wh': _L0_rec_in['Wh'], 'L0_rec_bh': _L0_rec_in['bh'], 'L0_rec_Wf': _L0_rec_in['Wf'], 'L0_rec_bf': _L0_rec_in['bf']}

def reference(r_numeric_feats, r_user_input, r_item_input, r_categorical_feats, L0_rec_user_emb, L0_rec_item_emb, L0_rec_cat_tables, L0_rec_num_W, L0_rec_num_b, L0_rec_Wc, L0_rec_bc, L0_rec_W0, L0_rec_b0, L0_rec_Wh, L0_rec_bh, L0_rec_Wf, L0_rec_bf):
    import jax
    import jax.numpy as jnp

    def _L0_rec_ref(user_input, item_input, numeric_feats, categorical_feats, user_emb, item_emb, cat_tables, num_W, num_b, Wc, bc, W0, b0, Wh, bh, Wf, bf):
        import jax, jax.numpy as jnp
        import numpy as np
        B = 2048
        EMB = 64
        N_NUM = 13
        N_CAT = 26
        CAT_VOCAB = 1250
        N_USERS = 12500
        N_ITEMS = 12500
        D = (2 + N_NUM + N_CAT) * EMB
        MLP_DIM = 1024
        N_MLP = 4
        L_CROSS = 4
        u = user_emb[user_input]
        it = item_emb[item_input]
        num_vec = numeric_feats[:, :, None] * num_W[None] + num_b[None]
        num_vec = num_vec.reshape(num_vec.shape[0], -1)
        cat_vec = jax.vmap(lambda tbl, idx: tbl[idx], in_axes=(0, 1), out_axes=1)(cat_tables, categorical_feats)
        cat_vec = cat_vec.reshape(cat_vec.shape[0], -1)
        x0 = jnp.concatenate([u, it, num_vec, cat_vec], axis=-1)
        x = x0
        for i in range(Wc.shape[0]):
            x = x0 * (x @ Wc[i] + bc[i]) + x
        h = jax.nn.relu(x0 @ W0 + b0)
        for i in range(Wh.shape[0]):
            h = jax.nn.relu(h @ Wh[i] + bh[i])
        x_final = jnp.concatenate([x, h], axis=-1)
        return jax.nn.sigmoid(x_final @ Wf + bf)
    y = _L0_rec_ref(r_user_input, r_item_input, r_numeric_feats, r_categorical_feats, L0_rec_user_emb, L0_rec_item_emb, L0_rec_cat_tables, L0_rec_num_W, L0_rec_num_b, L0_rec_Wc, L0_rec_bc, L0_rec_W0, L0_rec_b0, L0_rec_Wh, L0_rec_bh, L0_rec_Wf, L0_rec_bf)
    return y

_drawn_inputs = setup_inputs


def setup_inputs(seed=0):
    import zlib

    import numpy as np

    out = dict(_drawn_inputs(seed))
    spreads = {}
    factors = {'r_numeric_feats': 8.0,
     'L0_rec_user_emb': 8.0,
     'L0_rec_item_emb': 8.0,
     'L0_rec_cat_tables': 7.029,
     'L0_rec_num_W': 8.0,
     'L0_rec_num_b': 7.648,
     'L0_rec_Wc': 8.0,
     'L0_rec_bc': 8.0,
     'L0_rec_W0': 8.0,
     'L0_rec_b0': 64.0,
     'L0_rec_Wh': 8.0,
     'L0_rec_bh': 55.307,
     'L0_rec_Wf': 5.524}
    for name, (base, spread) in spreads.items():
        noise = np.random.default_rng([zlib.crc32(name.encode()), seed]).standard_normal(out[name].shape)
        drawn = base * np.exp(spread * noise) if base else spread * noise
        out[name] = jnp.asarray(drawn.astype(out[name].dtype))
    for name, factor in factors.items():
        out[name] = (out[name] * factor).astype(out[name].dtype)
    return out
```

```python
import concourse.bass as bass
from concourse import mybir
from contextlib import ExitStack

P = 128
BATCH, HALVES = 1024, 2
HB = BATCH // HALVES
EMB, N_NUM, N_CAT, VOCAB, N_ROWS = 64, 13, 26, 1250, 12500
D = (2 + N_NUM + N_CAT) * EMB
MLP = 1024
NT = 21
GW = 3 * P
TAIL = 20
CAT_TILES = list(range(12)) + [18]
UI_TILE = 19
NUM_TILES = [12, 13, 14, 15, 16, 17, TAIL]
GATHERED = CAT_TILES + [UI_TILE]
A_COLS = 7 * GW + MLP
A_CHUNKS = 16
A_CW = A_COLS // A_CHUNKS
NF = N_CAT + 2
NUMW = N_NUM * EMB
UW = 32
N_FOLD = 2 * N_NUM + 1


class Phase:

    def __init__(self, name, n_ab, c_tiles, widths, looped, kind):
        self.name, self.n_ab, self.c_tiles, self.widths = name, n_ab, c_tiles, widths
        self.looped, self.kind = looped, kind
        self.steps = 2 * n_ab + 1
        self.folded = "F" in c_tiles
        self.stacked = len(c_tiles) == 3


def make_plan():
    full = [GW] * 7
    mlp = [GW, GW, 2 * P]
    plan, step, group, tile, part = [], 0, 0, 0, 0
    fills = {"A": 0, "B": 0, "C": 0}
    for half in range(HALVES):
        x0, other = (0, 2) if half == 0 else (2, 0)
        off = 0
        for name, n_ab, c, widths, looped, kind, src, dst in (
                ("L0", 2, [18, 19, "F"], full, True, "cross", x0, 1),
                ("M0", 2, [18, 19, "F"], mlp, False, "relu", x0, (other, 0)),
                ("H0", 1, [6, 7], mlp, False, "relu", (other, 0), (other, 8)),
                ("H1", 1, [6, 7], mlp, False, "relu", (other, 8), (other, 0)),
                ("H2", 1, [6, 7], mlp, False, "relu_logit", (other, 0), (other, 8)),
                ("L1", 3, [18, 19, 20], full, True, "cross", 1, other),
                ("L2", 3, [18, 19, 20], full, True, "cross", other, 1),
                ("L3", 3, [18, 19, 20], [GW] * 5, False, "logit", 1, None)):
            ph = Phase(name, n_ab, c, widths, looped, kind)
            ph.half, ph.x0 = half, x0
            ph.src = src if isinstance(src, tuple) else (src, 0)
            ph.dst = dst if isinstance(dst, tuple) else (dst, 0)
            ph.step0, ph.group0, ph.tile0, ph.off = step, group, tile, off
            ph.fills0 = dict(fills)
            ph.index = len(plan)
            ph.part0 = part
            part += 0 if kind == "relu" else sum(widths) // P
            ph.dma = {"A": 1, "B": 1, "C": 2 if ph.folded else 1}
            plan.append(ph)
            step += ph.steps * len(widths)
            group += len(widths)
            tile += sum(widths) // P
            for b, n in (("A", n_ab), ("B", n_ab), ("C", 1)):
                fills[b] += n * ph.dma[b] * len(widths)
            if kind == "logit":
                for b, n in (("A", n_ab), ("B", n_ab), ("C", 1)):
                    fills[b] += n
            for g in range(len(widths)):
                off += group_size(ph, g)
    return plan, off


def group_width(ph, g):
    return 2 * P if (ph.kind == "logit" and g == 4) else ph.widths[g]


def group_size(ph, g):
    return P * (6 * ph.n_ab + (2 if ph.folded else len(ph.c_tiles))) * group_width(ph, g)


PLAN, STREAM = make_plan()


def build(nc, stream, num_rows, u_rows, cat, user, item, idx_in, idx_cst, fold, fold_t, feats, u_cst,
          cols, small, out):
    f32, f32r, i32 = mybir.dt.float32, mybir.dt.float32r, mybir.dt.int32
    ALU, ACT, AX = mybir.AluOpType, mybir.ActivationFunctionType, mybir.AxisListType

    with ExitStack() as ctx:
        def sb(name, shape, dt=f32):
            return ctx.enter_context(nc.sbuf_tensor(name, shape, dt))

        def sem(name):
            return ctx.enter_context(nc.semaphore(name))

        X = sb("X", [P, 3, NT, HB])
        F = sb("F", [P, HALVES, HB])
        x_hi, x_lo = sb("x_hi", [P, 3, HB], f32r), sb("x_lo", [P, 3, HB], f32r)
        w_hi, w_lo = sb("w_hi", [P, 3, GW], f32r), sb("w_lo", [P, 3, GW], f32r)
        raw = {b: sb("raw" + b, [P, 3, GW]) for b in "ABC"}
        A = sb("A", [P, A_COLS])
        U = sb("U", [P, NT, UW])
        G = sb("G", [P, 2, 4, P])
        acc = sb("acc", [P, HB])
        tmp = sb("tmp", [P, 2, HB])
        idx, idx_ok = sb("idx", [P, 8 * NF], i32), sb("idx_ok", [P, 8 * NF], i32)
        col = sb("col", [P, 8 * NT])
        sml = sb("sml", [UW, 3 * EMB])
        fold_T = sb("fold_T", [32, 7, P])
        ident = sb("ident", [P, P])
        ones = col[:, 8 * NT - 1:8 * NT]
        beta = sb("beta", [UW, 1])
        res = sb("res", [1, BATCH])
        bf = sb("bf", [1, 1])

        late = X[:, 2, :, :].rearrange("p t b -> p (t b)")
        rows_buf = [late[:, i * 7 * A_CW:(i + 1) * 7 * A_CW].rearrange("p (t c) -> p t c", t=7) for i in range(2)]
        u_at = NT * HB - 6 * NUMW
        u_c = late[:, u_at:u_at + 2 * NUMW].rearrange("p (t c) -> p t c", t=2)
        u_raw = late[:, u_at + 2 * NUMW:u_at + 4 * NUMW].rearrange("p (t c) -> p t c", t=2)
        u_prod = late[:, u_at + 4 * NUMW:u_at + 6 * NUMW].rearrange("p (t c) -> p t c", t=2)
        early = X[:, 1, :, :].rearrange("p t b -> p (t b)")
        fold_w = early[:, 0:7 * P].rearrange("p (t c) -> p t c", t=7)
        idx_c = early[:, 1024:1024 + 24 * NF].rearrange("p (t c) -> p t c", t=3)
        idx_f = early[:, 2048:2048 + 24 * NF].rearrange("p (t c) -> p t c", t=3)

        ps = ctx.enter_context(nc.psum_tensor("ps", [P, 8, HB], f32))

        s_const = sem("s_const")
        s_idx = sem("s_idx")
        s_idx_ok = sem("s_idx_ok")
        s_rows = [sem(f"s_rows{i}") for i in range(2)]
        s_a_mm = sem("s_a_mm")
        s_a = sem("s_a")
        s_uc = sem("s_uc")
        s_ur = [sem(f"s_ur{i}") for i in range(2)]
        s_u = sem("s_u")
        s_gather = [sem(f"s_gather{i}") for i in range(2)]
        s_tp = sem("s_tp")
        s_x0 = sem("s_x0")
        s_raw = {b: sem("s_raw" + b) for b in "ABC"}
        s_hi = sem("s_hi")
        s_lo = sem("s_lo")
        s_pe = sem("s_pe")
        s_out_tile = sem("s_out_tile")
        s_logit = sem("s_logit")
        s_res = sem("s_res")
        s_part = sem("s_part")
        s_dve = sem("s_dve")
        s_stored = sem("s_stored")
        block = ctx.enter_context(nc.Block())

        N_CONST = 8
        U_OPS = 7
        U_DONE = 2 + U_OPS * NT
        LO0, PE0, OUT0 = 6, 3, 1

        def groups(eng, ph, body):
            body(0, ph.group0 % 2)
            if ph.looped:
                with eng.Fori(0, 3) as r:
                    body(2 * r + 1, (ph.group0 + 1) % 2)
                    body(2 * r + 2, ph.group0 % 2)
            else:
                for g in range(1, len(ph.widths)):
                    body(g, (ph.group0 + g) % 2)

        def static(g):
            return isinstance(g, int)

        def width(ph, g):
            return group_width(ph, g) if static(g) else GW

        def out_tiles(ph, g):
            return ph.widths[g] // P if static(g) else 3

        def raw_count(ph, g, q, b):
            per = ph.dma[b]
            n = ph.n_ab if b != "C" else 1
            nth = pair["i"] if b != "C" else 0
            if ph.kind == "logit" and static(g) and g == 4:
                return 16 * (ph.fills0[b] + 4 * n * per + 2 * (nth + 1))
            return 16 * per * n * g + 16 * per * nth + 16 * (ph.fills0[b] + per)

        pair = {}

        def ab_loop(eng, ph, body, straight=False):
            pair["i"] = 0
            body(0, "A", True)
            body(1, "B", False)
            if ph.n_ab > 2 and not straight:
                with eng.Fori(1, ph.n_ab) as i:
                    pair["i"] = i
                    body(2 * i, "A", False)
                    body(2 * i + 1, "B", False)
            else:
                for i in range(1, ph.n_ab):
                    pair["i"] = i
                    body(2 * i, "A", False)
                    body(2 * i + 1, "B", False)

        prep_at = {}
        order = NUM_TILES + GATHERED
        prep_at[(0, "L0", 0, 0)] = NUM_TILES + GATHERED[0:3]
        for q in range(1, 5):
            prep_at[(0, "L0", 0, q)] = GATHERED[3 * q:3 * q + 3]
        later = list(GATHERED + NUM_TILES)
        for g in range(1, 5):
            for q in range(7):
                if later:
                    prep_at[(0, "L3", g, q)] = [later.pop(0)]
        prep_list = []
        for key, tiles in prep_at.items():
            for t in tiles:
                prep_list.append((0 if key[1] == "L0" else 1, t))
        prep_no = {ht: n for n, ht in enumerate(prep_list)}
        gather_list = [ht for ht in prep_list if ht[1] in GATHERED]
        gather_no = {ht: n for n, ht in enumerate(gather_list)}

        def preps(ph, g, q):
            if not (static(g) and static(q)):
                return []
            return [(0 if ph.name == "L0" else 1, t) for t in prep_at.get((ph.half, ph.name, g, q), [])]

        def prepared(ph, tiles):
            return max(prep_no[(ph.half, t)] for t in tiles) + 1

        @block.sync
        def _(sp):
            sp.dma_start(idx[:], idx_in).then_inc(s_idx, 16)
            sp.dma_start(idx_c, idx_cst).then_inc(s_idx, 16)
            sp.dma_start(F[:], feats).then_inc(s_const, 16)
            sp.dma_start(fold_w, fold).then_inc(s_const, 16)
            sp.dma_start(fold_T[:], fold_t).then_inc(s_const, 16)
            sp.dma_start(col[:], cols).then_inc(s_const, 16)
            sp.dma_start(sml[:], small[0:UW, 0:3 * EMB]).then_inc(s_const, 16)
            sp.dma_start(bf[:], small[0:1, 3 * EMB:3 * EMB + 1]).then_inc(s_const, 16)
            sp.dma_start(ident[:], small[:, 3 * EMB + 1:3 * EMB + 1 + P]).then_inc(s_const, 16)
            sp.dma_start(U[:], small[:, 3 * EMB + 1 + P:3 * EMB + 1 + P + NT * UW].rearrange("p (t c) -> p t c", t=NT)).then_inc(s_const, 16)
            for c in range(A_CHUNKS):
                if c >= 2:
                    sp.wait_ge(s_a_mm, c - 1)
                sp.dma_start(rows_buf[c % 2], num_rows[c]).then_inc(s_rows[c % 2], 16)
            for ph in PLAN:
                def sp_group(g, parity, ph=ph):
                    w = width(ph, g)
                    at = ph.off + (sum(group_size(ph, k) for k in range(g)) if static(g) else 0)
                    if not static(g):
                        at = group_size(ph, 0) * g + at

                    def fill(q, b, first):
                        sp.wait_ge(s_lo, 3 * ph.steps * g + 3 * q + (3 * ph.step0 + 3))
                        n = 2 if b == "C" and ph.folded else (len(ph.c_tiles) if b == "C" else 3)
                        src = stream[bass.ds(at + q * (3 * P * w), P * n * w)]
                        sp.dma_start(raw[b][:, 0:n, 0:w], src.rearrange("(p t c) -> p t c", p=P, t=n)
                                     ).then_inc(s_raw[b], 16)
                        if b == "C" and ph.folded:
                            if ph.index == 0 and static(g) and g == 0:
                                sp.wait_ge(s_a, A_CHUNKS)
                            a0 = 0 if ph.name == "L0" else 7 * GW
                            sp.dma_start(raw[b][:, 2, 0:w], A[:, bass.ds(GW * g + a0, w)]).then_inc(s_raw[b], 16)
                        if ph.kind == "logit" and g == 4:
                            if ph.half == 0 and static(q) and q == 0:
                                sp.wait_ge(s_u, U_DONE)
                            sp.dma_start(raw[b][:, :, w:w + UW], U[:, bass.ds(3 * q, 3), :]).then_inc(s_raw[b], 16)

                    ab_loop(sp, ph, fill, straight=ph.kind == "logit")
                    fill(2 * ph.n_ab, "C", False)

                groups(sp, ph, sp_group)
            sp.wait_ge(s_res, HALVES)
            sp.dma_start(out, res[:]).then_inc(s_stored, 16)
            sp.wait_ge(s_stored, 16)

        @block.gpsimd
        def _(pool):
            nc.gpsimd.dma_start(u_c, u_cst[:, 0:2]).then_inc(s_uc, 16)
            nc.gpsimd.dma_start(u_prod[:, 0], u_cst[:, 2]).then_inc(s_uc, 16)
            pool.wait_ge(s_idx_ok, 1)

            def gather(half):
                for h, t in gather_list:
                    if h != half:
                        continue
                    n = gather_no[(h, t)]
                    if n >= 2:
                        pool.wait_ge(s_tp, prep_no[gather_list[n - 2]] + 1)
                    for c in range(4):
                        for f in range(2):
                            if t == UI_TILE:
                                table, j = (user, item)[f], N_CAT + f
                            else:
                                table, j = cat, 2 * CAT_TILES.index(t) + f
                            at = (4 * h + c) * NF + j
                            nc.gpsimd.indirect_dma_start(
                                out=G[:, n % 2, c, f * EMB:(f + 1) * EMB], out_offset=None, in_=table,
                                in_offset=bass.IndirectOffsetOnAxis(ap=idx_ok[:, at:at + 1], axis=0)
                            ).then_inc(s_gather[n % 2], 16)

            gather(0)
            nc.gpsimd.dma_start(u_raw[:, 0], u_rows[0]).then_inc(s_ur[0], 16)
            pool.wait_ge(s_uc, 32)
            nc.gpsimd.tensor_tensor(u_c[:, 0], u_c[:, 0], u_prod[:, 0], ALU.mult).then_inc(s_u, 1)
            nc.gpsimd.tensor_tensor(u_c[:, 1], u_c[:, 1], u_prod[:, 0], ALU.mult).then_inc(s_u, 1)
            pool.wait_ge(s_u, 2)
            pool.wait_ge(s_const, 16 * N_CONST)
            for t in range(NT):
                pool.wait_ge(s_u, U_OPS * t + 2)
                if t + 1 < NT:
                    nc.gpsimd.dma_start(u_raw[:, (t + 1) % 2], u_rows[t + 1]).then_inc(s_ur[(t + 1) % 2], 16)
                pool.wait_ge(s_ur[t % 2], 16 * (t // 2 + 1))
                rows = u_raw[:, t % 2].unsqueeze(1).to_broadcast([P, 2, NUMW])
                nc.gpsimd.tensor_tensor(u_prod, rows, u_c, ALU.mult).then_inc(s_u, 1)
                half, n = NUMW // 2, 1
                while half >= N_NUM:
                    pool.wait_ge(s_u, U_OPS * t + 2 + n)
                    dst = U[:, t, 0:2 * N_NUM].rearrange("p (a c) -> p a c", a=2) if half == N_NUM else u_prod[:, :, 0:half]
                    nc.gpsimd.tensor_tensor(dst, u_prod[:, :, 0:half], u_prod[:, :, half:2 * half], ALU.add
                                            ).then_inc(s_u, 1)
                    half, n = half // 2, n + 1
            gather(1)

        @block.scalar
        def _(act):
            act.wait_ge(s_const, 16 * N_CONST)
            nc.scalar.copy(res[0:1, 0:1], bf[:])

            def prep(h, t, ph):
                n = prep_no[(h, t)]
                act.wait_ge(s_tp, n + 1)
                if n == NT:
                    act.wait_ge(s_out_tile, ph.tile0 + OUT0)
                nc.scalar.copy(X[:, 0 if h == 0 else 2, t, :], ps[:, 6 + n % 2, :]).then_inc(s_x0, 1)

            for ph in PLAN:
                buf, base = ph.src
                prev = PLAN[ph.index - 1] if ph.index else None

                def act_group(g, parity, ph=ph, buf=buf, base=base, prev=prev):
                    w = width(ph, g)

                    def step(q, b, first):
                        for h, t in preps(ph, g, q):
                            prep(h, t, ph)
                        s3 = 3 * ph.steps * g + 3 * q + 3 * ph.step0
                        tiles = ph.c_tiles if b == "C" else [0, 1, 2]
                        act.wait_ge(s_raw[b], raw_count(ph, g, q, b))
                        if static(g) and g == 0:
                            if ph.name in ("L0", "M0"):
                                ready = [t for t in ph.c_tiles[0:2]] if b == "C" else [3 * q, 3 * q + 1, 3 * q + 2]
                                act.wait_ge(s_x0, prepared(ph, ready))
                            elif b == "C":
                                act.wait_ge(s_out_tile, ph.tile0 + OUT0)
                            else:
                                writer = PLAN[ph.index - (5 if ph.name == "L1" else 1)]
                                act.wait_ge(s_out_tile, 3 * q + (3 + writer.tile0 + OUT0))
                        for j, t in enumerate(tiles):
                            end = j == len(tiles) - 1
                            act.wait_ge(s_pe, s3 + (j - 2 + PE0))
                            if t == "F":
                                src = F[:, ph.half, :]
                            elif b == "C":
                                src = X[:, buf, base + t, :]
                            else:
                                src = X[:, buf, bass.ds(3 * q + (base + t), 1), :].rearrange("p a b -> p (a b)")
                            nc.scalar.copy(x_hi[:, j, :], src).then_inc(s_hi, 1)
                            ww = w + UW if ph.kind == "logit" and w == 2 * P else w
                            nc.scalar.copy(w_hi[:, j, 0:ww], raw[b][:, j, 0:ww]).then_inc(s_hi, 1 if not end or j == 2 else 3)

                    ab_loop(act, ph, step, straight=bool(static(g) and any(k[0] == ph.half and k[1] == ph.name and k[2] == g for k in prep_at)))
                    step(2 * ph.n_ab, "C", False)

                groups(act, ph, act_group)
            for h in range(HALVES):
                act.wait_ge(s_logit, h + 1)
                nc.scalar.activation(res[0:1, h * HB:(h + 1) * HB], ps[0:1, 7 - h, :], ACT.Sigmoid,
                                     bias=bf[0:1, 0:1]).then_inc(s_res, 1)

        @block.vector
        def _(dve):
            chain = [0]

            def link(ins):
                chain[0] += 1
                ins.then_inc(s_dve, 1)
                dve.wait_ge(s_dve, chain[0])

            nc.vector.sem_inc(s_lo, LO0)
            nc.vector.sem_inc(s_out_tile, OUT0)
            dve.wait_ge(s_idx, 32)
            link(nc.vector.tensor_copy(idx_f[:, 0], idx[:]))
            link(nc.vector.scalar_tensor_tensor(idx_f[:, 1], idx_f[:, 0], 0.0, idx_c[:, 0], ALU.is_lt, ALU.mult))
            link(nc.vector.tensor_tensor(idx_f[:, 2], idx_f[:, 0], idx_f[:, 1], ALU.add))
            link(nc.vector.scalar_tensor_tensor(idx_f[:, 0], idx_f[:, 2], 0.0, idx_c[:, 1], ALU.max, ALU.min))
            nc.vector.tensor_tensor(idx_ok[:], idx_f[:, 0], idx_c[:, 2], ALU.add).then_inc(s_idx_ok, 1)
            dve.wait_ge(s_const, 16 * N_CONST)
            num, wf, bc = (sml[:, k * EMB:(k + 1) * EMB] for k in range(3))
            link(nc.vector.tensor_tensor(wf, wf, bc, ALU.mult))
            link(nc.vector.tensor_tensor(num, num, wf, ALU.mult))
            link(nc.vector.tensor_reduce(beta[:], num, AX.X, ALU.add))
            for c in range(A_CHUNKS):
                dve.wait_ge(s_a_mm, c + 1)
                nc.vector.tensor_copy(A[:, c * A_CW:(c + 1) * A_CW], ps[:, c % 2, 0:A_CW]).then_inc(s_a, 1)

            def bias(ph, t):
                at = {"L0": 0, "L1": NT, "L2": 2 * NT, "L3": 3 * NT, "M0": 4 * NT, "H0": 4 * NT + 8,
                      "H1": 4 * NT + 16, "H2": 4 * NT + 24}[ph.name]
                return col[:, bass.ds(at + t, 1)]

            def tile(b, k):
                return X[:, b, bass.ds(k, 1), :].rearrange("p a b -> p (a b)")

            def in_order(ph, k):
                return k if ph.kind != "logit" or k < 12 else k + 6

            def take(ph, g, m, parity):
                z = ps[:, 3 * parity + m, :]
                t = 3 * g + m
                if ph.kind == "relu":
                    if ph.name == "H0" and ph.half == 0 and t == 0:
                        dve.wait_ge(s_u, U_DONE)
                    nc.vector.tensor_scalar(tile(ph.dst[0], ph.dst[1] + t), z, bias(ph, t), 0.0, ALU.add, ALU.max
                                            ).then_inc(s_out_tile, 1)
                elif ph.kind == "relu_logit":
                    nc.vector.tensor_scalar(tile(ph.dst[0], ph.dst[1] + t), z, bias(ph, t), 0.0, ALU.add, ALU.max
                                            ).then_inc(s_part, 1)
                elif ph.kind == "logit" and g == 4 and m == 2:
                    nc.vector.scalar_tensor_tensor(tmp[0:UW, m % 2], z[0:UW, :], beta[:, 0:1], F[0:UW, ph.half, :],
                                                   ALU.add, ALU.mult).then_inc(s_part, 1)
                else:
                    k = in_order(ph, t) if ph.kind == "logit" else t
                    nc.vector.scalar_tensor_tensor(tmp[:, m % 2], z, bias(ph, k), tile(ph.x0, k),
                                                   ALU.add, ALU.mult).then_inc(s_part, 1)

            def finish(ph, g, m):
                t = 3 * g + m
                if ph.kind == "relu":
                    return
                dve.wait_ge(s_part, t + (ph.part0 + 1))
                if ph.kind == "cross":
                    nc.vector.tensor_tensor(tile(ph.dst[0], t), tmp[:, m % 2], tile(ph.src[0], t), ALU.add
                                            ).then_inc(s_out_tile, 1)
                    return
                dve.wait_ge(s_out_tile, t + (ph.tile0 + OUT0))
                if ph.kind == "relu_logit":
                    nc.vector.scalar_tensor_tensor(acc[:], tile(ph.dst[0], ph.dst[1] + t), wf_h(t), acc[:],
                                                   ALU.mult, ALU.add).then_inc(s_out_tile, 1)
                elif g == 4 and m == 2:
                    nc.vector.tensor_tensor(acc[0:UW, :], tmp[0:UW, m % 2], acc[0:UW, :], ALU.add
                                            ).then_inc(s_out_tile, 1)
                else:
                    nc.vector.scalar_tensor_tensor(acc[:], tmp[:, m % 2], wf_x(in_order(ph, t)), acc[:],
                                                   ALU.mult, ALU.add).then_inc(s_out_tile, 1)

            def wf_h(t):
                return col[:, 4 * NT + 32 + t:4 * NT + 33 + t]

            def wf_x(t):
                return col[:, 4 * NT + 40 + t:4 * NT + 41 + t]

            for ph in PLAN:
                buf, base = ph.src

                def dve_group(g, parity, ph=ph, buf=buf, base=base):
                    w = width(ph, g)
                    if static(g) and g == 0:
                        before = (PLAN[ph.index - 1], len(PLAN[ph.index - 1].widths) - 1) if ph.index else None
                    else:
                        before = (ph, g - 1)
                    if ph.name == "M0" and static(g) and g == 0:
                        if ph.half:
                            dve.wait_ge(s_logit, ph.half)
                        link(nc.vector.memset(acc[:], 0.0))

                    def step(q, b, first):
                        s3 = 3 * ph.steps * g + 3 * q + 3 * ph.step0
                        tiles = ph.c_tiles if b == "C" else [0, 1, 2]
                        for j, t in enumerate(tiles):
                            dve.wait_ge(s_hi, 6 * ph.steps * g + 6 * q + (6 * ph.step0 + 2 * j + 2))
                            take_now = static(q) and q == 1 and before is not None and j < out_tiles(*before)
                            if take_now:
                                bph, bg = before
                                if j == 0:
                                    dve.wait_ge(s_pe, 3 * ph.steps * g + (3 * ph.step0 + PE0))
                                take(bph, bg, j, 1 - parity)
                            stack = j == 2 and b == "C"
                            rows = slice(64, P) if stack else slice(0, P)
                            if t == "F":
                                src = F[rows, ph.half, :]
                            elif b == "C":
                                src = X[rows, buf, base + t, :]
                            else:
                                src = X[:, buf, bass.ds(3 * q + (base + t), 1), :].rearrange("p a b -> p (a b)")
                            dst = x_hi if stack else x_lo
                            nc.vector.tensor_tensor(dst[rows, j, :], src, x_hi[rows, j, :], ALU.subtract)
                            ww = w + UW if ph.kind == "logit" and w == 2 * P else w
                            nc.vector.tensor_tensor(w_lo[:, j, 0:ww], raw[b][:, j, 0:ww], w_hi[:, j, 0:ww],
                                                    ALU.subtract).then_inc(s_lo, 1 if not (j == 1 and len(tiles) == 2) else 2)
                            if take_now:
                                finish(bph, bg, j)

                    ab_loop(dve, ph, step)
                    step(2 * ph.n_ab, "C", False)

                groups(dve, ph, dve_group)
            last = PLAN[-1]
            dve.wait_ge(s_pe, 3 * (last.step0 + last.steps * 5) + PE0)
            for m in range(3):
                take(last, 4, m, (last.group0 + 4) % 2)
                finish(last, 4, m)

        @block.tensor
        def _(pe):
            nc.tensor.sem_inc(s_pe, PE0)
            pe.wait_ge(s_const, 16 * N_CONST)
            for c in range(A_CHUNKS):
                pe.wait_ge(s_rows[c % 2], 16 * (c // 2 + 1))
                if c >= 2:
                    pe.wait_ge(s_a, c - 1)
                for i in range(7):
                    mm = nc.tensor.matmul(ps[:, c % 2, 0:A_CW], fold_w[:, i, :], rows_buf[c % 2][:, i, :],
                                          start=(i == 0), stop=(i == 6))
                mm.then_inc(s_a_mm, 1)
            pe.wait_ge(s_a, A_CHUNKS)

            def prep(h, t):
                n = prep_no[(h, t)]
                if n >= 2:
                    pe.wait_ge(s_x0, n - 1)
                bank = ps[:, 6 + n % 2, :]
                if t in GATHERED:
                    k = gather_no[(h, t)]
                    pe.wait_ge(s_gather[k % 2], 128 * (k // 2 + 1))
                    for c in range(4):
                        mm = nc.tensor.transpose(bank[:, c * P:(c + 1) * P], G[:, k % 2, c, :], ident[:])
                else:
                    i = NUM_TILES.index(t)
                    mm = nc.tensor.matmul(bank, fold_T[:, i, :], F[0:32, h, :], start=True, stop=True)
                mm.then_inc(s_tp, 1)

            def logit(half):
                if half == 0:
                    pe.wait_ge(s_x0, len(prep_list))
                done = PLAN[(half + 1) * len(PLAN) // HALVES - 1]
                pe.wait_ge(s_out_tile, done.tile0 + 15 + OUT0)
                nc.tensor.matmul(ps[0:1, 7 - half, :], ones, acc[:], start=True, stop=True).then_inc(s_logit, 1)

            for ph in PLAN:
                def pe_group(g, parity, ph=ph):
                    mt = out_tiles(ph, g)
                    if not (ph.index == 0 and static(g) and g == 0):
                        if static(g):
                            before = (3 * (g - 1) if g else -(PLAN[ph.index - 1].widths[-1] // P))
                            pe.wait_ge(s_out_tile, ph.tile0 + before + OUT0)
                        else:
                            pe.wait_ge(s_out_tile, 3 * g + (ph.tile0 - 3 + OUT0))

                    def step(q, b, first):
                        for h, t in preps(ph, g, q):
                            prep(h, t)
                        if ph.half == 1 and ph.name == "L0" and static(g) and g == 0 and static(q) and q == 3:
                            logit(0)
                        tiles = ph.c_tiles if b == "C" else [0, 1, 2]
                        for j, t in enumerate(tiles):
                            pe.wait_ge(s_lo, 3 * ph.steps * g + 3 * q + (3 * ph.step0 + j + 1 + LO0))
                            stack = j == 2 and b == "C"
                            end = b == "C" and j == len(tiles) - 1
                            for m in range(mt):
                                bank = ps[:, 3 * parity + m, :]
                                cs = slice(m * P, (m + 1) * P)
                                nc.tensor.matmul(bank, w_hi[:, j, cs], x_hi[:, j, :], start=(first and j == 0), stop=False)
                                mm = nc.tensor.matmul(bank, w_lo[:, j, cs], x_hi[:, j, :], start=False, stop=(end and stack))
                                if not stack:
                                    mm = nc.tensor.matmul(bank, w_hi[:, j, cs], x_lo[:, j, :], start=False, stop=end)
                            mm.then_inc(s_pe, 2 if (end and j == 1) else 1)

                    ab_loop(pe, ph, step, straight=bool(static(g) and any(k[0] == ph.half and k[1] == ph.name and k[2] == g for k in prep_at)))
                    step(2 * ph.n_ab, "C", False)

                groups(pe, ph, pe_group)
            logit(1)


def kernel(**inputs):
    import numpy as np
    import concourse.bacc as bacc
    from concourse.bass_utils import run_bass_kernel_spmd as run

    v = {k.replace("L0_rec_", "").replace("r_", "", 1) if k.startswith("r_") else k.replace("L0_rec_", ""):
         np.asarray(a) for k, a in inputs.items()}
    f4 = np.float32

    def feature_rows():
        cat0 = (2 + N_NUM) * EMB
        cat_r = [np.arange(cat0 + P * k, cat0 + P * (k + 1)) for k in range(13)]
        num_r = [np.arange(P * (k + 1), P * (k + 2)) for k in range(6)]
        tail = np.arange(cat0 - EMB, cat0)
        return cat_r[:12] + num_r + [cat_r[12], np.arange(P), np.concatenate([tail, tail])]

    rows = feature_rows()
    allr = np.concatenate(rows)
    Wc, W0, Wh = v["Wc"], v["W0"], v["Wh"]

    def reorder(w, in_tiles, out_cols):
        return [w[r][:, out_cols] for r in in_tiles]

    parts = []

    def put(ph, tiles):
        at = 0
        for g in range(len(ph.widths)):
            w = group_width(ph, g)
            cut = [t[:, at:at + w] for t in tiles]
            at += w
            n = len(cut)
            for q in range(0, n, 3):
                parts.append(np.stack(cut[q:q + 3], axis=1).reshape(-1))

    for ph in PLAN[:len(PLAN) // 2]:
        if ph.name == "L0":
            put(ph, reorder(Wc[0], rows[:12] + rows[18:20], allr))
        elif ph.name == "M0":
            put(ph, reorder(W0, rows[:12] + rows[18:20], np.arange(MLP)))
        elif ph.name[0] == "H":
            put(ph, [Wh[int(ph.name[1])][P * k:P * (k + 1)] for k in range(8)])
        elif ph.name == "L3":
            put(ph, reorder(Wc[3], rows, np.concatenate(rows[:12] + rows[18:20])))
        else:
            put(ph, reorder(Wc[int(ph.name[1])], rows, allr))
    stream = np.concatenate(parts)
    assert stream.size == STREAM, (stream.size, STREAM)

    num = np.zeros((7 * P, A_COLS), f4)
    n0 = 2 * EMB
    num[:NUMW, :7 * GW] = Wc[0][n0:n0 + NUMW][:, allr]
    num[:NUMW, 7 * GW:] = W0[n0:n0 + NUMW]
    num_rows = np.ascontiguousarray(num.reshape(7, P, A_CHUNKS, A_CW).transpose(2, 1, 0, 3))
    num_ej = n0 + np.arange(NUMW).reshape(N_NUM, EMB).T.reshape(-1)
    u_rows = np.ascontiguousarray(Wc[3][allr][:, num_ej].reshape(NT, P, NUMW))

    idx = np.concatenate([v["categorical_feats"], v["user_input"][:, None], v["item_input"][:, None]], axis=1)
    idx = np.ascontiguousarray(idx.reshape(8, P, NF).transpose(1, 0, 2).reshape(P, 8 * NF))
    size = np.array([VOCAB] * N_CAT + [N_ROWS] * 2, f4)
    base = np.array([VOCAB * j for j in range(N_CAT)] + [0, 0], f4)
    idx_cst = np.ascontiguousarray(np.broadcast_to(np.stack([np.tile(x, 8) for x in (size, size - 1, base)]),
                                                   (P, 3, 8 * NF)))

    fold = np.zeros((P, 7, P), f4)
    fold_t = np.zeros((32, 7, P), f4)
    for j in range(N_NUM):
        r = slice(EMB * (j % 2), EMB * (j % 2) + EMB)
        for c in (0, 64):
            fold[r, j // 2, c + j] = v["num_W"][j]
            fold[r, j // 2, c + N_NUM] = v["num_b"][j]
        for rr in ([r] if j < 12 else [slice(0, 64), slice(64, 128)]):
            fold_t[j, j // 2, rr] = v["num_W"][j]
            fold_t[N_NUM, j // 2, rr] = v["num_b"][j]
    feats = np.zeros((P, BATCH), f4)
    for c in (0, 64):
        feats[c:c + N_NUM] = v["numeric_feats"].T
        feats[c + N_NUM:c + N_FOLD] = 1.0
    feats = feats.reshape(P, HALVES, HB)

    wf = v["Wf"][:, 0]
    u_cst = np.ascontiguousarray(np.broadcast_to(
        np.stack([v["num_W"].T.reshape(-1), v["num_b"].T.reshape(-1), wf[num_ej]]), (P, 3, NUMW)))

    cols = np.zeros((P, 8 * NT), f4)
    for i in range(4):
        cols[:, i * NT:(i + 1) * NT] = v["bc"][i][allr].reshape(NT, P).T
    cols[:, 4 * NT:4 * NT + 8] = v["b0"].reshape(8, P).T
    for i in range(3):
        cols[:, 4 * NT + 8 * (i + 1):4 * NT + 8 * (i + 2)] = v["bh"][i].reshape(8, P).T
    cols[:, 4 * NT + 32:4 * NT + 40] = wf[D:].reshape(8, P).T
    wf_cols = wf[:D][allr].reshape(NT, P).T
    cols[:, 4 * NT + 40:4 * NT + 40 + NT] = wf_cols

    cols[:, 8 * NT - 1] = 1.0

    small = np.zeros((P, 3 * EMB + 1 + P + NT * UW), f4)
    for r, name in ((slice(0, N_NUM), "num_W"), (slice(N_NUM, 2 * N_NUM), "num_b")):
        small[r, 0:EMB] = v[name]
        small[r, EMB:2 * EMB] = wf[n0:n0 + NUMW].reshape(N_NUM, EMB)
        small[r, 2 * EMB:3 * EMB] = v["bc"][3][n0:n0 + NUMW].reshape(N_NUM, EMB)
    small[0, 3 * EMB] = v["bf"][0]
    small[:, 3 * EMB + 1:3 * EMB + 1 + P] = np.eye(P, dtype=f4)
    small[:, 3 * EMB + 1 + P + 2 * N_NUM::UW] = wf_cols

    arrays = {
        "stream": stream, "num_rows": num_rows, "u_rows": u_rows,
        "cat": np.ascontiguousarray(v["cat_tables"].reshape(-1, EMB)),
        "user": np.ascontiguousarray(v["user_emb"]), "item": np.ascontiguousarray(v["item_emb"]),
        "idx_in": idx, "idx_cst": idx_cst, "fold": fold, "fold_t": fold_t, "feats": feats, "u_cst": u_cst,
        "cols": cols, "small": small,
    }
    nc = bacc.Bacc("TRN2", target_bir_lowering=False, num_devices=1)
    aps = [nc.dram_tensor(k, a.shape, mybir.dt.from_np(a.dtype), kind="ExternalInput").ap()
           for k, a in arrays.items()]
    o = nc.dram_tensor("logits", (1, BATCH), mybir.dt.float32, kind="ExternalOutput").ap()
    build(nc, *aps, o)
    r = run(nc, [arrays], core_ids=[0])
    return r.results[0]["logits"].reshape(BATCH, 1)
```

```python
import concourse.bass as bass
from concourse import mybir
from contextlib import ExitStack

P = 128
BATCH, HALVES = 1024, 2
HB = BATCH // HALVES
EMB, N_NUM, N_CAT, VOCAB, N_ROWS = 64, 13, 26, 1250, 12500
D = (2 + N_NUM + N_CAT) * EMB
MLP = 1024
NT = 21
GW = 3 * P
TAIL = 20
CAT_TILES = list(range(12)) + [18]
UI_TILE = 19
NUM_TILES = [12, 13, 14, 15, 16, 17, TAIL]
GATHERED = CAT_TILES + [UI_TILE]
GS = 3
A_COLS = 7 * GW + MLP
A_CHUNKS = 16
A_CW = A_COLS // A_CHUNKS
NF = N_CAT + 2
NUMW = N_NUM * EMB
UW = 32
N_FOLD = 2 * N_NUM + 1


class Phase:

    def __init__(self, name, k0, n_ab, c_tiles, widths, looped, kind, paired):
        self.name, self.k0, self.n_ab, self.c_tiles, self.widths = name, k0, n_ab, c_tiles, widths
        self.looped, self.kind, self.paired = looped, kind, paired
        self.steps = 2 * n_ab + (1 if c_tiles else 0)
        self.folded = "F" in c_tiles
        self.dma = {"A": 1, "B": 1, "C": 2 if self.folded else 1}


def make_plan():
    full, mlp, last = [GW] * 7, [GW, GW, 2 * P], [GW] * 5
    folded, plain, hidden = [18, 19, "F"], [18, 19, TAIL], [6, 7]
    plan, step, group, tile, part = [], 0, 0, 0, 0
    fills = {"A": 0, "B": 0, "C": 0}
    stream = 0
    for half in range(HALVES):
        x0, other = (0, 2) if half == 0 else (2, 0)
        first = ([("L0a", 0, 1, [], full, False, "partial", 0, x0, 1),
                  ("L0b", 6, 1, folded, full, True, "rest", 0, x0, 1)] if half == 0 else
                 [("L0", 0, 2, folded, full, True, "first", EMB, x0, 1)])
        off = 0
        for *args, src, dst in first + [
                ("M0", 0, 2, folded, mlp, False, "relu", 0, x0, (other, 0)),
                ("H0", 0, 1, hidden, mlp, False, "relu", 0, (other, 0), (other, 8)),
                ("H1", 0, 1, hidden, mlp, False, "relu", 0, (other, 8), (other, 0)),
                ("H2", 0, 1, hidden, mlp, False, "relu_logit", 0, (other, 0), (other, 8)),
                ("L1", 0, 3, plain, full, True, "cross", EMB, 1, other),
                ("L2", 0, 3, plain, full, True, "cross", EMB, other, 1),
                ("L3", 0, 3, plain, last, False, "logit", UW, 1, None)]:
            ph = Phase(*args)
            ph.half, ph.x0 = half, x0
            ph.src = src if isinstance(src, tuple) else (src, 0)
            ph.dst = dst if isinstance(dst, tuple) else (dst, 0)
            ph.index, ph.step0, ph.group0, ph.tile0, ph.part0 = len(plan), step, group, tile, part
            ph.fills0 = dict(fills)
            if ph.name == "L0b":
                ph.off, ph.sizes = 6 * P * GW, plan[-1].sizes
            else:
                ph.off = off
                tiles = 14 if ph.name == "L0a" else 6 * ph.n_ab + (2 if ph.folded else len(ph.c_tiles))
                ph.sizes = [P * tiles * group_width(ph, g) for g in range(len(ph.widths))]
                off += sum(ph.sizes)
            plan.append(ph)
            n = len(ph.widths)
            step += ph.steps * n
            group += n
            if ph.kind != "partial":
                tile += sum(ph.widths) // P
                part += 0 if ph.kind in ("relu", "first") else sum(ph.widths) // P
            for b, k in (("A", ph.n_ab), ("B", ph.n_ab), ("C", 1 if ph.c_tiles else 0)):
                fills[b] += k * (ph.dma[b] * n + (1 if ph.kind == "logit" else 0))
        stream = off
    return plan, stream


def group_width(ph, g):
    return 2 * P if (ph.kind == "logit" and g == 4) else ph.widths[g]


PLAN, STREAM = make_plan()


def build(nc, stream, num_rows, u_rows, cat, user, item, idx_in, idx_cst, fold, fold_t, feats, u_cst,
          cols, small, out):
    f32, f32r, i32 = mybir.dt.float32, mybir.dt.float32r, mybir.dt.int32
    ALU, ACT, AX = mybir.AluOpType, mybir.ActivationFunctionType, mybir.AxisListType

    with ExitStack() as ctx:
        def sb(name, shape, dt=f32):
            return ctx.enter_context(nc.sbuf_tensor(name, shape, dt))

        def sem(name):
            return ctx.enter_context(nc.semaphore(name))

        X = sb("X", [P, 3, NT, HB])
        F = sb("F", [P, HALVES, HB])
        x_hi, x_lo = sb("x_hi", [P, 3, HB], f32r), sb("x_lo", [P, 3, HB], f32r)
        w_hi, w_lo = sb("w_hi", [P, 3, GW], f32r), sb("w_lo", [P, 3, GW], f32r)
        raw = {b: sb("raw" + b, [P, 3, GW]) for b in "ABC"}
        A = sb("A", [P, A_COLS])
        U = sb("U", [P, NT, 2 * UW])
        G = sb("G", [P, GS, 4, P])
        acc = sb("acc", [P, HB])
        tmp = sb("tmp", [P, 2, HB])
        swap = sb("swap", [P, HB])
        idx, idx_ok = sb("idx", [P, 8 * NF], i32), sb("idx_ok", [P, 8 * NF], i32)
        col = sb("col", [P, 8 * NT])
        sml = sb("sml", [UW, 3 * EMB])
        fold_T = sb("fold_T", [32, 7, P])
        ident = sb("ident", [P, P])
        ones = col[:, 8 * NT - 1:8 * NT]
        beta = sb("beta", [UW, 1])
        res = tmp[0:1, :, :].rearrange("p a b -> p (a b)")
        bf = sb("bf", [1, 1])

        late = X[:, 2, :, :].rearrange("p t b -> p (t b)")
        rows_buf = [late[:, i * 7 * A_CW:(i + 1) * 7 * A_CW].rearrange("p (t c) -> p t c", t=7) for i in range(2)]
        u_at = NT * HB - 6 * NUMW
        u_c = late[:, u_at:u_at + 2 * NUMW].rearrange("p (t c) -> p t c", t=2)
        u_raw = late[:, u_at + 2 * NUMW:u_at + 4 * NUMW].rearrange("p (t c) -> p t c", t=2)
        u_prod = late[:, u_at + 4 * NUMW:u_at + 6 * NUMW].rearrange("p (t c) -> p t c", t=2)
        early = X[:, 1, :, :].rearrange("p t b -> p (t b)")
        fold_w = early[:, 0:7 * P].rearrange("p (t c) -> p t c", t=7)
        idx_c = early[:, 1024:1024 + 24 * NF].rearrange("p (t c) -> p t c", t=3)
        idx_f = early[:, 2048:2048 + 24 * NF].rearrange("p (t c) -> p t c", t=3)

        ps = ctx.enter_context(nc.psum_tensor("ps", [P, 8, HB], f32))

        s_const = sem("s_const")
        s_idx = sem("s_idx")
        s_idx_ok = sem("s_idx_ok")
        s_rows = [sem(f"s_rows{i}") for i in range(2)]
        s_a_mm = sem("s_a_mm")
        s_a = sem("s_a")
        s_uc = sem("s_uc")
        s_ur = [sem(f"s_ur{i}") for i in range(2)]
        s_b1 = sem("s_b1")
        s_u = sem("s_u")
        s_gather = [sem(f"s_gather{i}") for i in range(GS)]
        s_tp = sem("s_tp")
        s_x0 = sem("s_x0")
        s_raw = {b: sem("s_raw" + b) for b in "ABC"}
        s_hi = sem("s_hi")
        s_lo = sem("s_lo")
        s_pe = sem("s_pe")
        s_out_tile = sem("s_out_tile")
        s_early = sem("s_early")
        s_swap = sem("s_swap")
        s_sum = sem("s_sum")
        s_logit = sem("s_logit")
        s_res = sem("s_res")
        s_part = sem("s_part")
        s_dve = sem("s_dve")
        s_stored = sem("s_stored")
        block = ctx.enter_context(nc.Block())

        N_CONST = 8
        U_EARLY = 12
        U_DONE = 2 + 2 * NT + 1
        EARLY = 6
        LO0, PE0, OUT0 = 6, 3, 1

        def groups(eng, ph, body):
            body(0, ph.group0 % 2)
            if ph.looped:
                with eng.Fori(0, 2) as r:
                    body(2 * r + 1, (ph.group0 + 1) % 2)
                    body(2 * r + 2, ph.group0 % 2)
            for g in range(5 if ph.looped else 1, len(ph.widths)):
                body(g, (ph.group0 + g) % 2)

        def static(g):
            return isinstance(g, int)

        def width(ph, g):
            return group_width(ph, g) if static(g) else GW

        def out_tiles(ph, g):
            return ph.widths[g] // P if static(g) else 3

        def raw_count(ph, g, q, b):
            per = ph.dma[b]
            n = ph.n_ab if b != "C" else 1
            nth = turn["i"] if b != "C" else 0
            if ph.kind == "logit" and static(g) and g == 4:
                return 16 * (ph.fills0[b] + 4 * n * per + 2 * (nth + 1))
            return 16 * per * n * g + 16 * per * nth + 16 * (ph.fills0[b] + per)

        turn = {}

        def ab_loop(eng, ph, body, straight=False):
            turn["i"] = 0
            body(0, "A", True)
            body(1, "B", False)
            if ph.n_ab > 2 and not straight:
                with eng.Fori(1, ph.n_ab) as i:
                    turn["i"] = i
                    body(2 * i, "A", False)
                    body(2 * i + 1, "B", False)
            else:
                for i in range(1, ph.n_ab):
                    turn["i"] = i
                    body(2 * i, "A", False)
                    body(2 * i + 1, "B", False)

        prep_at = {}
        a_preps = {2: 0, 5: 1, 8: 2, 11: 3, 14: 4, 15: 5}
        for (g, q), i in {(1, 0): 6, (2, 0): 7, (2, 1): 8, (3, 0): 9, (4, 0): 10, (4, 1): 11, (5, 1): 12,
                          (6, 0): 13}.items():
            prep_at[(0, "L0a", g, q)] = [GATHERED[i]]
        for i, t in enumerate(GATHERED):
            prep_at[(0, "L3", 1 + 2 * i // 7, 2 * i % 7)] = [t]
        for i, t in enumerate(NUM_TILES):
            prep_at[(0, "L3", 1 + (4 * i + 1) // 7, (4 * i + 1) % 7)] = [t]
        prep_at = dict(sorted(prep_at.items(), key=lambda kv: (kv[0][1] == "L3", kv[0])))
        prep_list = [(0, t) for t in NUM_TILES + GATHERED[0:EARLY]]
        for key, tiles in prep_at.items():
            for t in tiles:
                prep_list.append((0 if key[1] == "L0a" else 1, t))
        prep_no = {ht: n for n, ht in enumerate(prep_list)}
        gather_list = [ht for ht in prep_list if ht[1] in GATHERED]
        gather_no = {ht: n for n, ht in enumerate(gather_list)}

        def preps(ph, g, q, at):
            if not (static(g) and static(q)):
                return []
            return [(0 if ph.name == "L0a" else 1, t) for t in at.get((ph.half, ph.name, g, q), [])]

        copy_at = {(h, n, g + (q + 1) // (2 if n == "L0a" else 7), (q + 1) % (2 if n == "L0a" else 7)): tiles
                   for (h, n, g, q), tiles in prep_at.items()}

        def prep_in(ph, g):
            return static(g) and any(k[0:3] == (ph.half, ph.name, g) for k in [*prep_at, *copy_at])

        def pair_width(ph, g):
            return ph.paired if static(g) and g == len(ph.widths) - 1 else 0

        def before_last(ph, g):
            for _ in range(2):
                g -= 1
                if g < 0:
                    if ph.index == 0:
                        return None
                    ph = PLAN[ph.index - 1]
                    g = len(ph.widths) - 1
            return ph, g

        def prepared(ph, tiles):
            return max(prep_no[(ph.half, t)] for t in tiles) + 1

        @block.sync
        def _(sp):
            sp.dma_start(idx[:], idx_in).then_inc(s_idx, 16)
            sp.dma_start(idx_c, idx_cst).then_inc(s_idx, 16)
            sp.dma_start(F[:], feats).then_inc(s_const, 16)
            sp.dma_start(fold_w, fold).then_inc(s_const, 16)
            sp.dma_start(fold_T[:], fold_t).then_inc(s_const, 16)
            sp.dma_start(col[:], cols).then_inc(s_const, 16)
            sp.dma_start(sml[:], small[0:UW, 0:3 * EMB]).then_inc(s_const, 16)
            sp.dma_start(bf[:], small[0:1, 3 * EMB:3 * EMB + 1]).then_inc(s_const, 16)
            sp.dma_start(ident[:], small[:, 3 * EMB + 1:3 * EMB + 1 + P]).then_inc(s_const, 16)
            sp.dma_start(U[:, :, 0:UW], small[:, 3 * EMB + 1 + P:3 * EMB + 1 + P + NT * UW].rearrange("p (t c) -> p t c", t=NT)).then_inc(s_const, 16)
            sp.dma_start(u_c, u_cst[:, 0:2]).then_inc(s_uc, 16)
            sp.dma_start(u_prod[:, 0], u_cst[:, 2]).then_inc(s_uc, 16)

            def load_u(t):
                if t >= 2:
                    sp.wait_ge(s_u, 2 * (t - 2) + 3)
                sp.dma_start(u_raw[:, t % 2], u_rows[t]).then_inc(s_ur[t % 2], 16)

            for c in range(A_CHUNKS):
                if c >= 2:
                    sp.wait_ge(s_a_mm, c - 1)
                sp.dma_start(rows_buf[c % 2], num_rows[c]).then_inc(s_rows[c % 2], 16)
                if c < U_EARLY:
                    load_u(c)
            for ph in PLAN:
                def sp_group(g, parity, ph=ph):
                    w = width(ph, g)
                    at = ph.off + sum(ph.sizes[:g]) if static(g) else ph.sizes[0] * g + ph.off
                    if ph.name == "L0a" and g >= 1:
                        load_u(U_EARLY - 1 + g)
                    if ph.name == "L0b" and static(g) and g == 0:
                        for t in range(U_EARLY + 6, NT):
                            load_u(t)

                    def fill(q, b, first):
                        sp.wait_ge(s_lo, 3 * ph.steps * g + 3 * q + (3 * ph.step0 + 3))
                        n = 2 if b == "C" and ph.folded else (len(ph.c_tiles) if b == "C" else 3)
                        src = stream[bass.ds(at + q * (3 * P * w), P * n * w)]
                        sp.dma_start(raw[b][:, 0:n, 0:w], src.rearrange("(p t c) -> p t c", p=P, t=n)
                                     ).then_inc(s_raw[b], 16)
                        if b == "C" and ph.folded:
                            if ph.name == "L0b" and static(g) and g == 0:
                                sp.wait_ge(s_a, A_CHUNKS)
                            a0 = 7 * GW if ph.name == "M0" else 0
                            sp.dma_start(raw[b][:, 2, 0:w], A[:, bass.ds(GW * g + a0, w)]).then_inc(s_raw[b], 16)
                        if ph.kind == "logit" and g == 4:
                            if ph.half == 0 and static(q) and q == 0:
                                sp.wait_ge(s_u, U_DONE)
                            sp.dma_start(raw[b][:, :, w:w + 2 * UW], U[:, bass.ds(3 * q, 3), :]).then_inc(s_raw[b], 16)

                    ab_loop(sp, ph, fill, straight=ph.kind == "logit")
                    if ph.c_tiles:
                        fill(2 * ph.n_ab, "C", False)

                groups(sp, ph, sp_group)
            sp.wait_ge(s_res, HALVES)
            sp.dma_start(out, res).then_inc(s_stored, 16)
            sp.wait_ge(s_stored, 16)

        @block.gpsimd
        def _(pool):
            pool.wait_ge(s_idx_ok, 1)

            def gather(half):
                for h, t in gather_list:
                    if h != half:
                        continue
                    n = gather_no[(h, t)]
                    if n >= GS:
                        pool.wait_ge(s_tp, prep_no[gather_list[n - GS]] + 1)
                    for c in range(4):
                        for f in range(2):
                            if t == UI_TILE:
                                table, j = (user, item)[f], N_CAT + f
                            else:
                                table, j = cat, 2 * CAT_TILES.index(t) + f
                            at = (4 * h + c) * NF + j
                            nc.gpsimd.indirect_dma_start(
                                out=G[:, n % GS, c, f * EMB:(f + 1) * EMB], out_offset=None, in_=table,
                                in_offset=bass.IndirectOffsetOnAxis(ap=idx_ok[:, at:at + 1], axis=0)
                            ).then_inc(s_gather[n % GS], 16)

            gather(0)
            gather(1)

        @block.scalar
        def _(act):
            act.wait_ge(s_const, 16 * N_CONST)
            nc.scalar.copy(swap[0:1, 0:1], bf[:])

            def prep(h, t, ph):
                n = prep_no[(h, t)]
                act.wait_ge(s_tp, n + 1)
                if n == NT:
                    act.wait_ge(s_out_tile, ph.tile0 + OUT0)
                nc.scalar.copy(X[:, 0 if h == 0 else 2, t, :], ps[:, 6 + n % 2, :]).then_inc(s_x0, 1)

            for t in NUM_TILES:
                prep(0, t, PLAN[0])
            for c in range(A_CHUNKS):
                act.wait_ge(s_a_mm, c + 1)
                nc.scalar.copy(A[:, c * A_CW:(c + 1) * A_CW], ps[:, c % 2, 0:A_CW]).then_inc(s_a, 1)
                if c in a_preps:
                    prep(0, GATHERED[a_preps[c]], PLAN[0])
            act.wait_ge(s_b1, 1)

            def take_early(g, parity):
                for m in range(3):
                    t = 3 * g + m
                    nc.scalar.activation(X[:, 1, t, :], ps[:, 3 * parity + m, :], ACT.Identity,
                                         bias=col[:, t:t + 1]).then_inc(s_early, 1)

            swaps = [0]

            def exchange(ph, parity):
                z, pw = ps[:, 3 * parity + 2, :], ph.paired
                act.wait_ge(s_out_tile, ph.tile0 + OUT0)
                if pw == EMB:
                    nc.scalar.copy(swap[pw:2 * pw, :], z[0:pw, :])
                nc.scalar.copy(swap[0:pw, :], z[pw:2 * pw, :]).then_inc(s_swap, 1)

            for ph in PLAN:
                buf, base = ph.src

                def act_group(g, parity, ph=ph, buf=buf, base=base):
                    w, pw = width(ph, g), pair_width(ph, g)
                    if static(g) and g == 0:
                        before = (PLAN[ph.index - 1], len(PLAN[ph.index - 1].widths) - 1) if ph.index else None
                    else:
                        before = (ph, g - 1)

                    def step(q, b, first):
                        for h, t in preps(ph, g, q, copy_at):
                            prep(h, t, ph)
                        s3 = 3 * ph.steps * g + 3 * q + 3 * ph.step0
                        tiles = ph.c_tiles if b == "C" else [0, 1, 2]
                        act.wait_ge(s_raw[b], raw_count(ph, g, q, b))
                        if static(g) and g == 0:
                            if ph.name in ("L0", "L0a", "L0b", "M0"):
                                ready = ph.c_tiles[0:2] if b == "C" else [ph.k0 + 3 * q + i for i in range(3)]
                                act.wait_ge(s_x0, prepared(ph, ready))
                            elif b == "C":
                                act.wait_ge(s_out_tile, ph.tile0 + OUT0)
                            else:
                                writer = PLAN[ph.index - (5 if ph.name == "L1" else 1)]
                                act.wait_ge(s_out_tile, 3 * q + (3 + writer.tile0 + OUT0))
                        if static(q) and q == 1 and before is not None:
                            bph, bg = before
                            if bph.kind == "partial" or pair_width(bph, bg):
                                act.wait_ge(s_pe, 3 * ph.steps * g + (3 * ph.step0 + PE0))
                                if bph.kind == "partial":
                                    take_early(bg, 1 - parity)
                                else:
                                    exchange(bph, 1 - parity)
                        for j, t in enumerate(tiles):
                            end = j == len(tiles) - 1
                            act.wait_ge(s_pe, s3 + (j - 2 + PE0))
                            if t == "F":
                                src = F[:, ph.half, :]
                            elif b == "C":
                                src = X[:, buf, base + t, :]
                            else:
                                src = X[:, buf, bass.ds(3 * q + (base + ph.k0 + t), 1), :].rearrange("p a b -> p (a b)")
                            nc.scalar.copy(x_hi[:, j, :], src).then_inc(s_hi, 1)
                            if pw:
                                ww, pair = 2 * P + pw, slice(2 * P + pw, 2 * P + 2 * pw)
                                nc.scalar.copy(w_lo[:, j, pair], raw[b][:, j, pair])
                            else:
                                ww = w
                            nc.scalar.copy(w_hi[:, j, 0:ww], raw[b][:, j, 0:ww]).then_inc(s_hi, 3 if end and j == 1 else 1)

                    ab_loop(act, ph, step, straight=prep_in(ph, g))
                    if ph.c_tiles:
                        step(2 * ph.n_ab, "C", False)

                groups(act, ph, act_group)
            last = PLAN[-1]
            act.wait_ge(s_pe, 3 * (last.step0 + last.steps * 5) + PE0)
            exchange(last, (last.group0 + 4) % 2)
            act.wait_ge(s_logit, HALVES)
            for h in range(HALVES):
                nc.scalar.activation(res[0:1, h * HB:(h + 1) * HB], ps[0:1, 7 - h, :], ACT.Sigmoid,
                                     bias=bf[0:1, 0:1]).then_inc(s_res, 1)

        @block.vector
        def _(dve):
            chain = [0]

            def link(ins):
                chain[0] += 1
                ins.then_inc(s_dve, 1)
                dve.wait_ge(s_dve, chain[0])

            nc.vector.sem_inc(s_lo, LO0)
            nc.vector.sem_inc(s_out_tile, OUT0)
            dve.wait_ge(s_idx, 32)
            link(nc.vector.tensor_copy(idx_f[:, 0], idx[:]))
            link(nc.vector.scalar_tensor_tensor(idx_f[:, 1], idx_f[:, 0], 0.0, idx_c[:, 0], ALU.is_lt, ALU.mult))
            link(nc.vector.tensor_tensor(idx_f[:, 2], idx_f[:, 0], idx_f[:, 1], ALU.add))
            link(nc.vector.scalar_tensor_tensor(idx_f[:, 0], idx_f[:, 2], 0.0, idx_c[:, 1], ALU.max, ALU.min))
            nc.vector.tensor_tensor(idx_ok[:], idx_f[:, 0], idx_c[:, 2], ALU.add).then_inc(s_idx_ok, 1)
            dve.wait_ge(s_const, 16 * N_CONST)
            num, wf, bc = (sml[:, k * EMB:(k + 1) * EMB] for k in range(3))
            link(nc.vector.tensor_tensor(wf, wf, bc, ALU.mult))
            link(nc.vector.tensor_tensor(num, num, wf, ALU.mult))
            link(nc.vector.tensor_reduce(beta[:], num, AX.X, ALU.add))
            nc.vector.tensor_scalar(col[:, 0:NT], col[:, 0:NT], 1.0, None, ALU.add).then_inc(s_b1, 1)
            dve.wait_ge(s_uc, 32)
            nc.vector.tensor_tensor(u_c[:, 0], u_c[:, 0], u_prod[:, 0], ALU.mult).then_inc(s_u, 1)
            nc.vector.tensor_tensor(u_c[:, 1], u_c[:, 1], u_prod[:, 0], ALU.mult).then_inc(s_u, 1)

            def make_u(t):
                dve.wait_ge(s_ur[t % 2], 16 * (t // 2 + 1))
                dve.wait_ge(s_u, 2 * t + 2)
                rows = u_raw[:, t % 2].unsqueeze(1).to_broadcast([P, 2, NUMW])
                nc.vector.tensor_tensor(u_prod, rows, u_c, ALU.mult).then_inc(s_u, 1)
                dve.wait_ge(s_u, 2 * t + 3)
                nc.vector.tensor_reduce(U[:, t, 0:2 * N_NUM], u_prod.rearrange("p a (j e) -> p (a j) e", e=EMB),
                                        AX.X, ALU.add).then_inc(s_u, 1)

            for t in range(U_EARLY):
                make_u(t)

            def bias(ph, t):
                at = {"L0": 0, "L0b": 0, "L1": NT, "L2": 2 * NT, "L3": 3 * NT, "M0": 4 * NT, "H0": 4 * NT + 8,
                      "H1": 4 * NT + 16, "H2": 4 * NT + 24}[ph.name]
                return col[:, bass.ds(at + t, 1)]

            def tile(b, k):
                return X[:, b, bass.ds(k, 1), :].rearrange("p a b -> p (a b)")

            def in_order(ph, k):
                return k if ph.kind != "logit" or k < 12 else k + 6

            def halves(ph, parity):
                n = 2 * EMB if ph.paired == EMB else ph.paired
                pairs[0] += 1
                dve.wait_ge(s_swap, pairs[0])
                nc.vector.tensor_tensor(swap[0:n, :], ps[0:n, 3 * parity + 2, :], swap[0:n, :], ALU.add
                                        ).then_inc(s_sum, 1)

            pairs = [0]

            def take(ph, g, m, parity):
                z = ps[:, 3 * parity + m, :]
                if m == 2 and pair_width(ph, g):
                    z = swap[:]
                    dve.wait_ge(s_sum, pairs[0])
                t = 3 * g + m
                if ph.kind == "first":
                    nc.vector.scalar_tensor_tensor(tile(1, t), z, bias(ph, t), tile(ph.x0, t), ALU.add, ALU.mult
                                                   ).then_inc(s_out_tile, 1)
                elif ph.kind == "rest":
                    nc.vector.tensor_tensor(tmp[:, m % 2], z, tile(1, t), ALU.add).then_inc(s_part, 1)
                elif ph.kind == "relu":
                    nc.vector.tensor_scalar(tile(ph.dst[0], ph.dst[1] + t), z, bias(ph, t), 0.0, ALU.add, ALU.max
                                            ).then_inc(s_out_tile, 1)
                elif ph.kind == "relu_logit":
                    nc.vector.tensor_scalar(tile(ph.dst[0], ph.dst[1] + t), z, bias(ph, t), 0.0, ALU.add, ALU.max
                                            ).then_inc(s_part, 1)
                elif ph.kind == "logit" and g == 4 and m == 2:
                    nc.vector.scalar_tensor_tensor(tmp[0:UW, m % 2], z[0:UW, :], beta[:, 0:1], F[0:UW, ph.half, :],
                                                   ALU.add, ALU.mult).then_inc(s_part, 1)
                else:
                    k = in_order(ph, t) if ph.kind == "logit" else t
                    nc.vector.scalar_tensor_tensor(tmp[:, m % 2], z, bias(ph, k), tile(ph.x0, k),
                                                   ALU.add, ALU.mult).then_inc(s_part, 1)

            def finish(ph, g, m):
                t = 3 * g + m
                if ph.kind in ("relu", "first"):
                    return
                dve.wait_ge(s_part, t + (ph.part0 + 1))
                if ph.kind == "rest":
                    nc.vector.tensor_tensor(tile(1, t), tmp[:, m % 2], tile(ph.x0, t), ALU.mult
                                            ).then_inc(s_out_tile, 1)
                    return
                if ph.kind == "cross":
                    nc.vector.tensor_tensor(tile(ph.dst[0], t), tmp[:, m % 2], tile(ph.src[0], t), ALU.add
                                            ).then_inc(s_out_tile, 1)
                    return
                dve.wait_ge(s_out_tile, t + (ph.tile0 + OUT0))
                if ph.kind == "relu_logit":
                    nc.vector.scalar_tensor_tensor(acc[:], tile(ph.dst[0], ph.dst[1] + t), wf_h(t), acc[:],
                                                   ALU.mult, ALU.add).then_inc(s_out_tile, 1)
                elif g == 4 and m == 2:
                    nc.vector.tensor_tensor(acc[0:UW, :], tmp[0:UW, m % 2], acc[0:UW, :], ALU.add
                                            ).then_inc(s_out_tile, 1)
                else:
                    nc.vector.scalar_tensor_tensor(acc[:], tmp[:, m % 2], wf_x(in_order(ph, t)), acc[:],
                                                   ALU.mult, ALU.add).then_inc(s_out_tile, 1)

            def wf_h(t):
                return col[:, 4 * NT + 32 + t:4 * NT + 33 + t]

            def wf_x(t):
                return col[:, 4 * NT + 40 + t:4 * NT + 41 + t]

            for ph in PLAN:
                buf, base = ph.src

                def dve_group(g, parity, ph=ph, buf=buf, base=base):
                    w, pw = width(ph, g), pair_width(ph, g)
                    if static(g) and g == 0:
                        before = (PLAN[ph.index - 1], len(PLAN[ph.index - 1].widths) - 1) if ph.index else None
                    else:
                        before = (ph, g - 1)
                    if ph.name == "L0a" and g >= 1:
                        make_u(U_EARLY - 1 + g)
                    if ph.name == "L0b" and static(g) and g == 0:
                        for t in range(U_EARLY + 6, NT):
                            make_u(t)
                        dve.wait_ge(s_u, U_DONE - 1)
                        nc.vector.tensor_copy(U[:, :, UW:2 * UW], U[:, :, 0:UW]).then_inc(s_u, 1)
                    if ph.name == "M0" and static(g) and g == 0:
                        if ph.half:
                            dve.wait_ge(s_logit, ph.half)
                        link(nc.vector.memset(acc[:], 0.0))

                    def step(q, b, first):
                        s3 = 3 * ph.steps * g + 3 * q + 3 * ph.step0
                        tiles = ph.c_tiles if b == "C" else [0, 1, 2]
                        for j, t in enumerate(tiles):
                            dve.wait_ge(s_hi, 6 * ph.steps * g + 6 * q + (6 * ph.step0 + 2 * j + 2))
                            take_now = (static(q) and q == 1 and before is not None and before[0].kind != "partial"
                                        and j < out_tiles(*before))
                            if take_now:
                                bph, bg = before
                                if j == 0:
                                    dve.wait_ge(s_pe, 3 * ph.steps * g + (3 * ph.step0 + PE0))
                                if ph.name == "L0b" and static(bg) and bg == 0 and j == 0:
                                    dve.wait_ge(s_early, NT)
                                take(bph, bg, j, 1 - parity)
                                if j == 1 and pair_width(bph, bg):
                                    halves(bph, 1 - parity)
                            stack = j == 2 and b == "C"
                            rows = slice(64, P) if stack else slice(0, P)
                            if t == "F":
                                src = F[rows, ph.half, :]
                            elif b == "C":
                                src = X[rows, buf, base + t, :]
                            else:
                                src = X[:, buf, bass.ds(3 * q + (base + ph.k0 + t), 1), :].rearrange("p a b -> p (a b)")
                            dst = x_hi if stack else x_lo
                            nc.vector.tensor_tensor(dst[rows, j, :], src, x_hi[rows, j, :], ALU.subtract)
                            ww = 2 * P + pw if pw else w
                            if pw:
                                nc.vector.tensor_tensor(w_hi[:, j, ww:ww + pw], raw[b][:, j, ww:ww + pw],
                                                        w_hi[:, j, 2 * P:ww], ALU.subtract)
                            nc.vector.tensor_tensor(w_lo[:, j, 0:ww], raw[b][:, j, 0:ww], w_hi[:, j, 0:ww],
                                                    ALU.subtract).then_inc(s_lo, 1 if not (j == 1 and len(tiles) == 2) else 2)
                            if take_now:
                                finish(bph, bg, j)

                    ab_loop(dve, ph, step)
                    if ph.c_tiles:
                        step(2 * ph.n_ab, "C", False)

                groups(dve, ph, dve_group)
            last = PLAN[-1]
            dve.wait_ge(s_pe, 3 * (last.step0 + last.steps * 5) + PE0)
            for m in range(3):
                if m == 2:
                    halves(last, (last.group0 + 4) % 2)
                take(last, 4, m, (last.group0 + 4) % 2)
                finish(last, 4, m)

        @block.tensor
        def _(pe):
            nc.tensor.sem_inc(s_pe, PE0)
            def prep(h, t):
                n = prep_no[(h, t)]
                if n >= 2:
                    pe.wait_ge(s_x0, n - 1)
                bank = ps[:, 6 + n % 2, :]
                if t in GATHERED:
                    k = gather_no[(h, t)]
                    pe.wait_ge(s_gather[k % GS], 128 * (k // GS + 1))
                    for c in range(4):
                        mm = nc.tensor.transpose(bank[:, c * P:(c + 1) * P], G[:, k % GS, c, :], ident[:])
                else:
                    i = NUM_TILES.index(t)
                    mm = nc.tensor.matmul(bank, fold_T[:, i, :], F[0:32, h, :], start=True, stop=True)
                mm.then_inc(s_tp, 1)

            pe.wait_ge(s_const, 16 * N_CONST)
            for t in NUM_TILES:
                prep(0, t)
            for c in range(A_CHUNKS):
                pe.wait_ge(s_rows[c % 2], 16 * (c // 2 + 1))
                if c >= 2:
                    pe.wait_ge(s_a, c - 1)
                for i in range(7):
                    mm = nc.tensor.matmul(ps[:, c % 2, 0:A_CW], fold_w[:, i, :], rows_buf[c % 2][:, i, :],
                                          start=(i == 0), stop=(i == 6))
                mm.then_inc(s_a_mm, 1)
                if c in a_preps:
                    prep(0, GATHERED[a_preps[c]])
            pe.wait_ge(s_a, A_CHUNKS)

            def logit(half):
                if half == 0:
                    pe.wait_ge(s_x0, len(prep_list))
                done = [ph for ph in PLAN if ph.half == half][-1]
                pe.wait_ge(s_out_tile, done.tile0 + 15 + OUT0)
                nc.tensor.matmul(ps[0:1, 7 - half, :], ones, acc[:], start=True, stop=True).then_inc(s_logit, 1)

            for ph in PLAN:
                def pe_group(g, parity, ph=ph):
                    mt = out_tiles(ph, g)
                    pw = pair_width(ph, g)
                    if not static(g):
                        pe.wait_ge(s_out_tile, 3 * g + (ph.tile0 - 3 + OUT0))
                    elif before_last(ph, g) is not None:
                        bph, bg = before_last(ph, g)
                        if bph.kind == "partial":
                            pe.wait_ge(s_early, 3 * bg + 3)
                        else:
                            pe.wait_ge(s_out_tile, bph.tile0 + 3 * bg + out_tiles(bph, bg) + OUT0)

                    def step(q, b, first):
                        for h, t in preps(ph, g, q, prep_at):
                            prep(h, t)
                        if ph.half == 1 and ph.name == "L0" and static(g) and g == 0 and static(q) and q == 3:
                            logit(0)
                        tiles = ph.c_tiles if b == "C" else [0, 1, 2]
                        for j, t in enumerate(tiles):
                            pe.wait_ge(s_lo, 3 * ph.steps * g + 3 * q + (3 * ph.step0 + j + 1 + LO0))
                            stack = j == 2 and b == "C"
                            last_step = b == "C" or (not ph.c_tiles and q == 2 * ph.n_ab - 1)
                            end = last_step and j == len(tiles) - 1
                            if ph.name == "L0b" and static(g) and g == 0 and b == "C" and j == 0:
                                pe.wait_ge(s_early, NT)
                            for m in range(mt):
                                bank = ps[:, 3 * parity + m, :]
                                cs = slice(m * P, (m + 1) * P)
                                paired = m == 2 and pw
                                mm = nc.tensor.matmul(bank, w_hi[:, j, cs], x_hi[:, j, :], start=(first and j == 0),
                                                      stop=bool(end and stack and paired))
                                if not paired:
                                    mm = nc.tensor.matmul(bank, w_lo[:, j, cs], x_hi[:, j, :], start=False,
                                                          stop=(end and stack))
                                if not stack:
                                    mm = nc.tensor.matmul(bank, (w_lo if paired else w_hi)[:, j, cs], x_lo[:, j, :],
                                                          start=False, stop=end)
                            mm.then_inc(s_pe, 2 if (end and j == 1) else 1)

                    ab_loop(pe, ph, step, straight=prep_in(ph, g))
                    if ph.c_tiles:
                        step(2 * ph.n_ab, "C", False)

                groups(pe, ph, pe_group)
            logit(1)


def kernel(**inputs):
    import numpy as np
    import concourse.bacc as bacc
    from concourse.bass_utils import run_bass_kernel_spmd as run

    v = {k.replace("L0_rec_", "").replace("r_", "", 1) if k.startswith("r_") else k.replace("L0_rec_", ""):
         np.asarray(a) for k, a in inputs.items()}
    f4 = np.float32

    def feature_rows():
        cat0 = (2 + N_NUM) * EMB
        cat_r = [np.arange(cat0 + P * k, cat0 + P * (k + 1)) for k in range(13)]
        num_r = [np.arange(P * (k + 1), P * (k + 2)) for k in range(6)]
        tail = np.arange(cat0 - EMB, cat0)
        return cat_r[:12] + num_r + [cat_r[12], np.arange(P), np.concatenate([tail, tail])]

    rows = feature_rows()
    allr = np.concatenate(rows)
    Wc, W0, Wh = v["Wc"], v["W0"], v["Wh"]

    def reorder(w, in_tiles, out_cols):
        return [w[r][:, out_cols] for r in in_tiles]

    parts = []

    def put(ph, tiles):
        at = 0
        for g in range(len(ph.widths)):
            w = group_width(ph, g)
            cut = [t[:, at:at + w] for t in tiles]
            at += w
            n = len(cut)
            for q in range(0, n, 3):
                parts.append(np.stack(cut[q:q + 3], axis=1).reshape(-1))

    for ph in [ph for ph in PLAN if ph.half == 1]:
        if ph.name == "L0":
            put(ph, reorder(Wc[0], rows[:12] + rows[18:20], allr))
        elif ph.name == "M0":
            put(ph, reorder(W0, rows[:12] + rows[18:20], np.arange(MLP)))
        elif ph.name[0] == "H":
            put(ph, [Wh[int(ph.name[1])][P * k:P * (k + 1)] for k in range(8)])
        elif ph.name == "L3":
            put(ph, reorder(Wc[3], rows, np.concatenate(rows[:12] + rows[18:20])))
        else:
            put(ph, reorder(Wc[int(ph.name[1])], rows, allr))
    stream = np.concatenate(parts)
    assert stream.size == STREAM, (stream.size, STREAM)

    num = np.zeros((7 * P, A_COLS), f4)
    n0 = 2 * EMB
    num[:NUMW, :7 * GW] = Wc[0][n0:n0 + NUMW][:, allr]
    num[:NUMW, 7 * GW:] = W0[n0:n0 + NUMW]
    num_rows = np.ascontiguousarray(num.reshape(7, P, A_CHUNKS, A_CW).transpose(2, 1, 0, 3))
    u_rows = np.ascontiguousarray(Wc[3][allr][:, n0:n0 + NUMW].reshape(NT, P, NUMW))

    idx = np.concatenate([v["categorical_feats"], v["user_input"][:, None], v["item_input"][:, None]], axis=1)
    idx = np.ascontiguousarray(idx.reshape(8, P, NF).transpose(1, 0, 2).reshape(P, 8 * NF))
    size = np.array([VOCAB] * N_CAT + [N_ROWS] * 2, f4)
    base = np.array([VOCAB * j for j in range(N_CAT)] + [0, 0], f4)
    idx_cst = np.ascontiguousarray(np.broadcast_to(np.stack([np.tile(x, 8) for x in (size, size - 1, base)]),
                                                   (P, 3, 8 * NF)))

    fold = np.zeros((P, 7, P), f4)
    fold_t = np.zeros((32, 7, P), f4)
    for j in range(N_NUM):
        r = slice(EMB * (j % 2), EMB * (j % 2) + EMB)
        for c in (0, 64):
            fold[r, j // 2, c + j] = v["num_W"][j]
            fold[r, j // 2, c + N_NUM] = v["num_b"][j]
        for rr in ([r] if j < 12 else [slice(0, 64), slice(64, 128)]):
            fold_t[j, j // 2, rr] = v["num_W"][j]
            fold_t[N_NUM, j // 2, rr] = v["num_b"][j]
    feats = np.zeros((P, BATCH), f4)
    for c in (0, 64):
        feats[c:c + N_NUM] = v["numeric_feats"].T
        feats[c + N_NUM:c + N_FOLD] = 1.0
    feats = feats.reshape(P, HALVES, HB)

    wf = v["Wf"][:, 0]
    u_cst = np.ascontiguousarray(np.broadcast_to(
        np.stack([v["num_W"].reshape(-1), v["num_b"].reshape(-1), wf[n0:n0 + NUMW]]), (P, 3, NUMW)))

    cols = np.zeros((P, 8 * NT), f4)
    for i in range(4):
        cols[:, i * NT:(i + 1) * NT] = v["bc"][i][allr].reshape(NT, P).T
    cols[:, 4 * NT:4 * NT + 8] = v["b0"].reshape(8, P).T
    for i in range(3):
        cols[:, 4 * NT + 8 * (i + 1):4 * NT + 8 * (i + 2)] = v["bh"][i].reshape(8, P).T
    cols[:, 4 * NT + 32:4 * NT + 40] = wf[D:].reshape(8, P).T
    wf_cols = wf[:D][allr].reshape(NT, P).T
    cols[:, 4 * NT + 40:4 * NT + 40 + NT] = wf_cols

    cols[:, 8 * NT - 1] = 1.0

    small = np.zeros((P, 3 * EMB + 1 + P + NT * UW), f4)
    for r, name in ((slice(0, N_NUM), "num_W"), (slice(N_NUM, 2 * N_NUM), "num_b")):
        small[r, 0:EMB] = v[name]
        small[r, EMB:2 * EMB] = wf[n0:n0 + NUMW].reshape(N_NUM, EMB)
        small[r, 2 * EMB:3 * EMB] = v["bc"][3][n0:n0 + NUMW].reshape(N_NUM, EMB)
    small[0, 3 * EMB] = v["bf"][0]
    small[:, 3 * EMB + 1:3 * EMB + 1 + P] = np.eye(P, dtype=f4)
    small[:, 3 * EMB + 1 + P + 2 * N_NUM::UW] = wf_cols

    arrays = {
        "stream": stream, "num_rows": num_rows, "u_rows": u_rows,
        "cat": np.ascontiguousarray(v["cat_tables"].reshape(-1, EMB)),
        "user": np.ascontiguousarray(v["user_emb"]), "item": np.ascontiguousarray(v["item_emb"]),
        "idx_in": idx, "idx_cst": idx_cst, "fold": fold, "fold_t": fold_t, "feats": feats, "u_cst": u_cst,
        "cols": cols, "small": small,
    }
    nc = bacc.Bacc("TRN2", target_bir_lowering=False, num_devices=1)
    aps = [nc.dram_tensor(k, a.shape, mybir.dt.from_np(a.dtype), kind="ExternalInput").ap()
           for k, a in arrays.items()]
    o = nc.dram_tensor("logits", (1, BATCH), mybir.dt.float32, kind="ExternalOutput").ap()
    build(nc, *aps, o)
    r = run(nc, [arrays], core_ids=[0])
    return r.results[0]["logits"].reshape(BATCH, 1)
```

```python
import concourse.bass as bass
from concourse import mybir
from contextlib import ExitStack

P = 128
BATCH, HALVES = 1024, 2
HB = BATCH // HALVES
EMB, N_NUM, N_CAT, VOCAB, N_ROWS = 64, 13, 26, 1250, 12500
D = (2 + N_NUM + N_CAT) * EMB
MLP = 1024
NT = 21
GW = 3 * P
TAIL = 20
CAT_TILES = list(range(12)) + [18]
UI_TILE = 19
NUM_TILES = [12, 13, 14, 15, 16, 17, TAIL]
GATHERED = CAT_TILES + [UI_TILE]
BIAS = {"L0": 0, "L0b": 0, "L1": NT, "L2": 2 * NT, "L3": 3 * NT, "M0": 4 * NT, "H0": 4 * NT + 8,
        "H1": 4 * NT + 16, "H2": 4 * NT + 24}
WF_H, WF_X = 4 * NT + 32, 4 * NT + 40
NUM_COL = WF_X + NT
N_COLS = NUM_COL + 15
GS = 3
A_COLS = 7 * GW + MLP
A_CHUNKS = 16
A_CW = A_COLS // A_CHUNKS
NF = N_CAT + 2
NUMW = N_NUM * EMB
UW = 32
N_FOLD = 2 * N_NUM + 1


class Phase:

    def __init__(self, name, k0, n_ab, c_tiles, widths, looped, kind, paired):
        self.name, self.k0, self.n_ab, self.c_tiles, self.widths = name, k0, n_ab, c_tiles, widths
        self.looped, self.kind, self.paired = looped, kind, paired
        self.uses = 6 * n_ab + len(c_tiles)
        self.folded = "F" in c_tiles
        self.dma = {"A": 1, "B": 1, "C": 2 if self.folded else 1}


def make_plan():
    full, mlp, last = [GW] * 7, [GW, GW, 2 * P], [GW] * 5
    folded, plain, hidden = [18, 19, "F"], [18, 19, TAIL], [6, 7]
    plan, use, group, tile, part = [], 0, 0, 0, 0
    fills = {"A": 0, "B": 0, "C": 0}
    for half in range(HALVES):
        x0, other = (0, 2) if half == 0 else (2, 0)
        first = ([("L0a", 0, 1, [], full, False, "partial", 0, x0, 1),
                  ("L0b", 6, 1, folded, full, True, "rest", 0, x0, 1)] if half == 0 else
                 [("L0", 0, 2, folded, full, True, "first", EMB, x0, 1)])
        off = 0
        for *args, src, dst in first + [
                ("M0", 0, 2, folded, mlp, False, "relu", 0, x0, (other, 0)),
                ("H0", 0, 1, hidden, mlp, False, "relu", 0, (other, 0), (other, 8)),
                ("H1", 0, 1, hidden, mlp, False, "relu", 0, (other, 8), (other, 0)),
                ("H2", 0, 1, hidden, mlp, False, "relu_logit", 0, (other, 0), (other, 8)),
                ("L1", 0, 3, plain, full, True, "cross", EMB, 1, other),
                ("L2", 0, 3, plain, full, True, "cross", EMB, other, 1),
                ("L3", 0, 3, plain, last, False, "logit", UW, 1, None)]:
            ph = Phase(*args)
            ph.half, ph.x0 = half, x0
            ph.src = src if isinstance(src, tuple) else (src, 0)
            ph.dst = dst if isinstance(dst, tuple) else (dst, 0)
            ph.index, ph.use0, ph.group0, ph.tile0, ph.part0 = len(plan), use, group, tile, part
            ph.fills0 = dict(fills)
            if ph.name == "L0b":
                ph.off, ph.sizes = 6 * P * GW, plan[-1].sizes
            else:
                ph.off = off
                tiles = 14 if ph.name == "L0a" else 6 * ph.n_ab + (2 if ph.folded else len(ph.c_tiles))
                ph.sizes = [P * tiles * group_width(ph, g) for g in range(len(ph.widths))]
                off += sum(ph.sizes)
            plan.append(ph)
            n = len(ph.widths)
            use += ph.uses * n
            group += n
            if ph.kind != "partial":
                tile += sum(ph.widths) // P
                part += 0 if ph.kind in ("relu", "first") else sum(ph.widths) // P
            for b, k in (("A", ph.n_ab), ("B", ph.n_ab), ("C", 1 if ph.c_tiles else 0)):
                fills[b] += k * (ph.dma[b] * n + (1 if ph.kind == "logit" else 0))
    return plan, off


def group_width(ph, g):
    return 2 * P if (ph.kind == "logit" and g == 4) else ph.widths[g]


PLAN, STREAM = make_plan()


def build(nc, stream, num_rows, u_rows, cat, user, item, idx_in, idx_cst, fold, feats, feats_wide, u_cst,
          cols, small, out):
    f32, f32r, i32 = mybir.dt.float32, mybir.dt.float32r, mybir.dt.int32
    ALU, ACT, AX = mybir.AluOpType, mybir.ActivationFunctionType, mybir.AxisListType

    with ExitStack() as ctx:
        def sb(name, shape, dt=f32):
            return ctx.enter_context(nc.sbuf_tensor(name, shape, dt))

        def sem(name):
            return ctx.enter_context(nc.semaphore(name))

        X = sb("X", [P, 3, NT, HB])
        F = sb("F", [P, HALVES, HB])
        x_hi, x_lo = sb("x_hi", [P, 3, HB], f32r), sb("x_lo", [P, 3, HB], f32r)
        w_hi, w_lo = sb("w_hi", [P, 3, GW], f32r), sb("w_lo", [P, 3, GW], f32r)
        raw = {b: sb("raw" + b, [P, 3, GW]) for b in "ABC"}
        A = sb("A", [P, A_COLS])
        U = sb("U", [P, NT, 2 * UW])
        G = sb("G", [P, GS, 4, P])
        acc = sb("acc", [P, HB])
        tmp = sb("tmp", [P, 2, HB])
        swap = sb("swap", [P, HB])
        idx, idx_ok = sb("idx", [P, 8 * NF], i32), sb("idx_ok", [P, 8 * NF], i32)
        col = sb("col", [P, N_COLS])
        sml = sb("sml", [UW, 3 * EMB])
        ident = sb("ident", [P, P])
        ones = col[:, N_COLS - 1:N_COLS]
        beta = sb("beta", [UW, 1])
        u_prod = tmp[:, :, :].rearrange("p a b -> p (a b)")[:, 0:NUMW]
        res = tmp[0:1, :, :].rearrange("p a b -> p (a b)")
        bf = sb("bf", [1, 1])

        late = X[:, 2, :, :].rearrange("p t b -> p (t b)")
        rows_buf = [late[:, i * 7 * A_CW:(i + 1) * 7 * A_CW].rearrange("p (t c) -> p t c", t=7) for i in range(3)]
        u_0 = 16 * HB
        u_c = late[:, u_0:u_0 + 2 * NUMW].rearrange("p (t c) -> p t c", t=2)
        u_raw = late[:, u_0 + 2 * NUMW:u_0 + 3 * NUMW]
        early = X[:, 1, :, :].rearrange("p t b -> p (t b)")
        fold_w = early[:, 0:7 * P].rearrange("p (t c) -> p t c", t=7)
        idx_c = early[:, 1024:1024 + 3 * NF].rearrange("p (t c) -> p t c", t=3)
        idx_f = early[:, 2048:2048 + 24 * NF].rearrange("p (t c) -> p t c", t=3)

        ps = ctx.enter_context(nc.psum_tensor("ps", [P, 8, HB], f32))

        s_fold = sem("s_fold")
        s_const = sem("s_const")
        s_late = sem("s_late")
        s_idx = sem("s_idx")
        s_idx_ok = sem("s_idx_ok")
        s_rows = [sem(f"s_rows{i}") for i in range(3)]
        s_a_mm = sem("s_a_mm")
        s_a = sem("s_a")
        s_uc = sem("s_uc")
        s_ur = sem("s_ur")
        s_b1 = sem("s_b1")
        s_feats = sem("s_feats")
        s_u = sem("s_u")
        s_gather = [sem(f"s_gather{i}") for i in range(GS)]
        s_tp = sem("s_tp")
        s_x0 = sem("s_x0")
        s_raw = {b: sem("s_raw" + b) for b in "ABC"}
        s_hi = sem("s_hi")
        s_lo = sem("s_lo")
        s_pe = sem("s_pe")
        s_out_tile = sem("s_out_tile")
        s_early = sem("s_early")
        s_swap = sem("s_swap")
        s_sum = sem("s_sum")
        s_logit = sem("s_logit")
        s_res = sem("s_res")
        s_part = sem("s_part")
        s_dve = sem("s_dve")
        s_stored = sem("s_stored")
        block = ctx.enter_context(nc.Block())

        N_CONST = 3
        U_EARLY = 3
        U_DONE = 3 + 4 * NT + 1
        EARLY = 6
        LO0, PE0, OUT0 = 6, 3, 1

        def groups(eng, ph, body):
            body(0, ph.group0 % 2)
            if ph.looped:
                with eng.Fori(0, 2) as r:
                    body(2 * r + 1, (ph.group0 + 1) % 2)
                    body(2 * r + 2, ph.group0 % 2)
            for g in range(5 if ph.looped else 1, len(ph.widths)):
                body(g, (ph.group0 + g) % 2)

        def static(g):
            return isinstance(g, int)

        def slot(ph, g, j):
            return (ph.uses * g + j) % 3 if static(g) else j

        def width(ph, g):
            return group_width(ph, g) if static(g) else GW

        def out_tiles(ph, g):
            return ph.widths[g] // P if static(g) else 3

        def raw_count(ph, g, q, b):
            per = ph.dma[b]
            n = ph.n_ab if b != "C" else 1
            nth = turn["i"] if b != "C" else 0
            if ph.kind == "logit" and static(g) and g == 4:
                return 16 * (ph.fills0[b] + 4 * n * per + 2 * (nth + 1))
            return 16 * per * n * g + 16 * per * nth + 16 * (ph.fills0[b] + per)

        u_slots = [("L0a", g, 0) for g in range(1, 7)] + [("L0b", 0, 0), ("M0", 1, 0)]
        u_slots += [("H0", 0, 1), ("H0", 1, 1), ("H1", 0, 1), ("H1", 1, 1), ("H2", 0, 1)]
        u_slots += [("L1", 0, 0), ("L1", 0, 2), ("L1", 0, 4), ("L1", 5, 3), ("L1", 5, 5)]
        u_at = {slot: U_EARLY + i for i, slot in enumerate(u_slots)}
        assert U_EARLY + len(u_slots) == NT

        def u_tile(ph, g, q):
            return u_at.get((ph.name, g, q)) if static(g) and static(q) and ph.half == 0 else None

        def u_in(ph, g):
            return ph.half == 0 and ph.name == "L1" and static(g) and g in (0, 5)

        def taken_tile(before, q, j):
            if not static(q) or q == 0 or before is None:
                return None
            at, n = 3 * (q - 1) + j, out_tiles(*before)
            if n == 2 or before[0].kind == "partial":
                return at if at < n else None
            return at // 2 if at in (0, 2, 4) else None

        u_loads = {6: 0, 9: 1, 12: 2}
        turn = {}

        def ab_loop(eng, ph, body, straight=False):
            turn["i"] = 0
            body(0, "A", True)
            body(1, "B", False)
            if ph.n_ab > 2 and not straight:
                with eng.Fori(1, ph.n_ab) as i:
                    turn["i"] = i
                    body(2 * i, "A", False)
                    body(2 * i + 1, "B", False)
            else:
                for i in range(1, ph.n_ab):
                    turn["i"] = i
                    body(2 * i, "A", False)
                    body(2 * i + 1, "B", False)

        prep_at = {}
        a_preps = {3: 0, 6: 1, 9: 2, 12: 3, 15: 4}
        for (g, q), i in {(0, 0): 5, (1, 1): 6, (2, 0): 7, (2, 1): 8, (3, 1): 9, (4, 0): 10, (5, 0): 11,
                          (5, 1): 12, (6, 0): 13}.items():
            prep_at[(0, "L0a", g, q)] = [GATHERED[i]]
        for i, t in enumerate(GATHERED):
            prep_at[(0, "L3", 1 + 2 * i // 7, 2 * i % 7)] = [t]
        num_at = {(0, "L0a", i // 2, i % 2): t for i, t in enumerate(NUM_TILES, 6)}
        num_at.update({(0, "L3", 2 + (3 * i) // 7, (3 * i) % 7): t for i, t in enumerate(NUM_TILES)})
        prep_at = dict(sorted(prep_at.items(), key=lambda kv: (kv[0][1] == "L3", kv[0])))
        prep_list = [(0, t) for t in GATHERED[0:EARLY - 1]]
        for key, tiles in prep_at.items():
            for t in tiles:
                prep_list.append((0 if key[1] == "L0a" else 1, t))
        prep_no = {ht: n for n, ht in enumerate(prep_list)}
        gather_list = [ht for ht in prep_list if ht[1] in GATHERED]
        gather_no = {ht: n for n, ht in enumerate(gather_list)}

        def preps(ph, g, q, at):
            if not (static(g) and static(q)):
                return []
            return [(0 if ph.name == "L0a" else 1, t) for t in at.get((ph.half, ph.name, g, q), [])]

        copy_at = {(h, n, g + (q + 1) // (2 if n == "L0a" else 7), (q + 1) % (2 if n == "L0a" else 7)): tiles
                   for (h, n, g, q), tiles in prep_at.items()}

        def prep_in(ph, g):
            return static(g) and any(k[0:3] == (ph.half, ph.name, g) for k in [*prep_at, *copy_at, *num_at])

        def pair_width(ph, g):
            return ph.paired if static(g) and g == len(ph.widths) - 1 else 0

        def before_last(ph, g):
            for _ in range(2):
                g -= 1
                if g < 0:
                    if ph.index == 0:
                        return None
                    ph = PLAN[ph.index - 1]
                    g = len(ph.widths) - 1
            return ph, g

        def prepared(ph, tiles):
            return max(prep_no[(ph.half, t)] for t in tiles) + 1

        @block.sync
        def _(sp):
            sp.dma_start(idx[:], idx_in).then_inc(s_idx, 16)
            sp.dma_start(idx_c, idx_cst).then_inc(s_idx, 16)
            sp.dma_start(fold_w, fold).then_inc(s_fold, 16)

            def load_constants():
                sp.dma_start(col[:], cols).then_inc(s_const, 16)
                sp.dma_start(sml[:], small[0:UW, 0:3 * EMB]).then_inc(s_const, 16)
                sp.dma_start(bf[:], small[0:1, 3 * EMB:3 * EMB + 1]).then_inc(s_const, 16)

            def load_u(t):
                if t > 0:
                    sp.wait_ge(s_u, 4 * t + 2)
                sp.dma_start(u_raw, u_rows[t]).then_inc(s_ur, 16)

            for c in range(A_CHUNKS):
                if c >= 3:
                    sp.wait_ge(s_a_mm, c - 2)
                sp.dma_start(rows_buf[c % 3][:, 0:6], num_rows[c][:, 0:6]).then_inc(s_rows[c % 3], 16)
                sp.dma_start(rows_buf[c % 3][0:EMB, 6], num_rows[c][0:EMB, 6]).then_inc(s_rows[c % 3], 16)
                if c == 0:
                    sp.dma_start(ident[:], small[:, 3 * EMB + 1:3 * EMB + 1 + P]).then_inc(s_fold, 16)
                if c == 2:
                    load_constants()
                if c == 3:
                    sp.dma_start(u_c[:, 0], u_cst[:, 0]).then_inc(s_uc, 16)
                    sp.dma_start(u_prod, u_cst[:, 2]).then_inc(s_uc, 16)
                if c == 4:
                    sp.dma_start(u_c[:, 1], u_cst[:, 1]).then_inc(s_uc, 16)
                if c in u_loads:
                    load_u(u_loads[c])
            for ph in PLAN:
                def sp_group(g, parity, ph=ph):
                    w = width(ph, g)
                    at = ph.off + sum(ph.sizes[:g]) if static(g) else ph.sizes[0] * g + ph.off
                    if ph.kind == "logit" and ph.half == 0 and g == 1:
                        sp.wait_ge(s_out_tile, ph.tile0 + OUT0)
                        sp.dma_start(X[:, 2, 12:18, :], feats_wide[1][:, 0:6]).then_inc(s_feats, 16)
                        sp.dma_start(X[:, 2, TAIL, :], feats_wide[1][:, 6]).then_inc(s_feats, 16)

                    if ph.name == "L0a" and g == 2:
                        sp.dma_start(F[:], feats).then_inc(s_late, 16)
                        sp.dma_start(X[:, 0, 12:18, :], feats_wide[0][:, 0:6]).then_inc(s_feats, 16)
                        sp.dma_start(X[:, 0, TAIL, :], feats_wide[0][:, 6]).then_inc(s_feats, 16)

                    def fill(q, b, first):
                        if static(q) and q and u_tile(ph, g, q - 1) is not None:
                            load_u(u_tile(ph, g, q - 1))
                        back = 1 if ph.uses == 8 or (ph.name == "L1" and static(g) and g == 0) else 0
                        if ph.name == "L0a" or (ph.name == "L0b" and static(g) and g == 0):
                            back = 3
                        if not (static(q) and q < 2) and b != "C":
                            back = 3
                        sp.wait_ge(s_lo, ph.uses * g + 3 * q + (ph.use0 + back))
                        n = 2 if b == "C" and ph.folded else (len(ph.c_tiles) if b == "C" else 3)
                        src = stream[bass.ds(at + q * (3 * P * w), P * n * w)]
                        sp.dma_start(raw[b][:, 0:n, 0:w], src.rearrange("(p t c) -> p t c", p=P, t=n)
                                     ).then_inc(s_raw[b], 16)
                        if b == "C" and ph.folded:
                            if ph.name == "L0b" and static(g) and g == 0:
                                sp.wait_ge(s_a, A_CHUNKS)
                            a0 = 7 * GW if ph.name == "M0" else 0
                            sp.dma_start(raw[b][:, 2, 0:w], A[:, bass.ds(GW * g + a0, w)]).then_inc(s_raw[b], 16)
                        if ph.kind == "logit" and g == 4:
                            if ph.half == 0 and static(q) and q == 0:
                                sp.wait_ge(s_u, U_DONE)
                            sp.dma_start(raw[b][:, :, w:w + 2 * UW], U[:, bass.ds(3 * q, 3), :]).then_inc(s_raw[b], 16)

                    ab_loop(sp, ph, fill, straight=ph.kind == "logit" or u_in(ph, g))
                    if ph.c_tiles:
                        fill(2 * ph.n_ab, "C", False)

                groups(sp, ph, sp_group)
            sp.wait_ge(s_res, HALVES)
            sp.dma_start(out, res).then_inc(s_stored, 16)
            sp.wait_ge(s_stored, 16)

        @block.gpsimd
        def _(pool):
            pool.wait_ge(s_idx_ok, 1)

            def gather(half):
                for h, t in gather_list:
                    if h != half:
                        continue
                    n = gather_no[(h, t)]
                    if n >= GS:
                        pool.wait_ge(s_tp, prep_no[gather_list[n - GS]] + 1)
                    for c in range(4):
                        for f in range(2):
                            if t == UI_TILE:
                                table, j = (user, item)[f], N_CAT + f
                            else:
                                table, j = cat, 2 * CAT_TILES.index(t) + f
                            at = (4 * h + c) * NF + j
                            nc.gpsimd.indirect_dma_start(
                                out=G[:, n % GS, c, f * EMB:(f + 1) * EMB], out_offset=None, in_=table,
                                in_offset=bass.IndirectOffsetOnAxis(ap=idx_ok[:, at:at + 1], axis=0)
                            ).then_inc(s_gather[n % GS], 16)

            gather(0)
            gather(1)

        @block.scalar
        def _(act):
            act.wait_ge(s_const, 16 * N_CONST)
            nc.scalar.copy(swap[0:1, 0:1], bf[:])

            def prep(h, t, ph):
                n = prep_no[(h, t)]
                act.wait_ge(s_tp, n + 1)
                if n == len(GATHERED):
                    act.wait_ge(s_out_tile, ph.tile0 + OUT0)
                nc.scalar.copy(X[:, 0 if h == 0 else 2, t, :], ps[:, 6 + n % 2, :]).then_inc(s_x0, 1)

            def numeric(ph, t):
                i = NUM_TILES.index(t)
                nth = 0 if ph.name == "L0a" else 1
                act.wait_ge(s_feats, 32 * (nth + 1))
                x = X[:, 2 * nth, t, :]
                nc.scalar.activation(x, x, ACT.Identity, scale=col[:, NUM_COL + i:NUM_COL + i + 1],
                                     bias=col[:, NUM_COL + 7 + i:NUM_COL + 8 + i])

            def copy_a(c):
                act.wait_ge(s_a_mm, c + 1)
                nc.scalar.copy(A[:, c * A_CW:(c + 1) * A_CW], ps[:, 3 + c % 2, 0:A_CW]).then_inc(s_a, 1)
                if c in a_preps:
                    prep(0, GATHERED[a_preps[c]], PLAN[0])

            for c in range(A_CHUNKS - 1):
                copy_a(c)
            act.wait_ge(s_b1, 1)

            def take_early(g, m, parity):
                t = 3 * g + m
                nc.scalar.activation(X[:, 1, t, :], ps[:, 3 * parity + m, :], ACT.Identity,
                                     bias=col[:, t:t + 1]).then_inc(s_early, 1)

            def take_relu(ph, g, m, parity):
                t = 3 * g + m
                if t == 0 and ph.name == "M0":
                    act.wait_ge(s_out_tile, ph.tile0 + OUT0)
                b = BIAS[ph.name] + t
                nc.scalar.activation(X[:, ph.dst[0], ph.dst[1] + t, :], ps[:, 3 * parity + m, :], ACT.Relu,
                                     bias=col[:, b:b + 1]).then_inc(s_part if ph.kind == "relu_logit" else s_out_tile, 1)

            def exchange(ph, parity):
                z, pw = ps[:, 3 * parity + 2, :], ph.paired
                act.wait_ge(s_out_tile, ph.tile0 + OUT0)
                if pw == EMB:
                    nc.scalar.copy(swap[pw:2 * pw, :], z[0:pw, :])
                nc.scalar.copy(swap[0:pw, :], z[pw:2 * pw, :]).then_inc(s_swap, 1)

            for ph in PLAN:
                buf, base = ph.src

                def act_group(g, parity, ph=ph, buf=buf, base=base):
                    if ph.name == "L0b" and static(g) and g == 0:
                        act.wait_ge(s_late, 16)
                    w, pw = width(ph, g), pair_width(ph, g)
                    if static(g) and g == 0:
                        before = (PLAN[ph.index - 1], len(PLAN[ph.index - 1].widths) - 1) if ph.index else None
                    else:
                        before = (ph, g - 1)

                    def step(q, b, first):
                        j_prep = 2 if ph.index == 0 and static(g) and (g, q) == (0, 1) else 0
                        if static(g) and static(q) and (ph.half, ph.name, g, q) in num_at:
                            numeric(ph, num_at[(ph.half, ph.name, g, q)])
                        s3 = ph.uses * g + 3 * q + ph.use0
                        tiles = ph.c_tiles if b == "C" else [0, 1, 2]
                        act.wait_ge(s_raw[b], raw_count(ph, g, q, b))
                        if static(g) and g == 0:
                            if ph.name in ("L0", "L0a", "L0b", "M0"):
                                ready = ph.c_tiles[0:2] if b == "C" else [ph.k0 + 3 * q + i for i in range(j_prep or 3)]
                                act.wait_ge(s_x0, prepared(ph, ready))
                            elif b == "C":
                                act.wait_ge(s_out_tile, ph.tile0 + OUT0)
                            else:
                                writer = PLAN[ph.index - (5 if ph.name == "L1" else 1)]
                                act.wait_ge(s_out_tile, 3 * q + (3 + writer.tile0 + OUT0))
                        if static(q) and q == 1 and before is not None:
                            bph, bg = before
                            if bph.kind in ("partial", "relu", "relu_logit") or pair_width(bph, bg):
                                act.wait_ge(s_pe, ph.uses * g + (ph.use0 + PE0))
                                if bph.kind not in ("partial", "relu", "relu_logit"):
                                    exchange(bph, 1 - parity)
                        for j, t in enumerate(tiles):
                            if j == j_prep:
                                for h, x0_tile in preps(ph, g, q, copy_at):
                                    prep(h, x0_tile, ph)
                                if j:
                                    act.wait_ge(s_x0, EARLY)
                            m = taken_tile(before, q, j)
                            if m is not None and before[0].kind == "partial":
                                take_early(before[1], m, 1 - parity)
                            elif m is not None and before[0].kind in ("relu", "relu_logit"):
                                take_relu(*before, m, 1 - parity)
                            act.wait_ge(s_pe, s3 + (j - 2 + PE0))
                            if t == "F":
                                src = F[:, ph.half, :]
                            elif b == "C":
                                src = X[:, buf, base + t, :]
                            else:
                                src = X[:, buf, bass.ds(3 * q + (base + ph.k0 + t), 1), :].rearrange("p a b -> p (a b)")
                            k = slot(ph, g, j)
                            nc.scalar.copy(x_hi[:, k, :], src).then_inc(s_hi, 1)
                            if pw:
                                ww, pair = 2 * P + pw, slice(2 * P + pw, 2 * P + 2 * pw)
                                nc.scalar.copy(w_lo[:, k, pair], raw[b][:, j, pair])
                            else:
                                ww = w
                            nc.scalar.copy(w_hi[:, k, 0:ww], raw[b][:, j, 0:ww]).then_inc(s_hi, 1)

                        if ph.index == 0 and static(g) and g == 0 and static(q) and q == 0:
                            copy_a(A_CHUNKS - 1)

                    ab_loop(act, ph, step, straight=prep_in(ph, g))
                    if ph.c_tiles:
                        step(2 * ph.n_ab, "C", False)

                groups(act, ph, act_group)
            last = PLAN[-1]
            act.wait_ge(s_pe, last.use0 + 5 * last.uses + PE0)
            exchange(last, (last.group0 + 4) % 2)
            act.wait_ge(s_logit, HALVES)
            for h in range(HALVES):
                nc.scalar.activation(res[0:1, h * HB:(h + 1) * HB], ps[0:1, 7 - h, :], ACT.Sigmoid,
                                     bias=bf[0:1, 0:1]).then_inc(s_res, 1)

        @block.vector
        def _(dve):
            chain = [0]

            def link(ins):
                chain[0] += 1
                ins.then_inc(s_dve, 1)
                dve.wait_ge(s_dve, chain[0])

            nc.vector.sem_inc(s_lo, LO0)
            nc.vector.sem_inc(s_out_tile, OUT0)
            dve.wait_ge(s_idx, 32)
            size, top, base = (idx_c[:, i].unsqueeze(1).to_broadcast([P, 8, NF]) for i in range(3))
            n, wrap, at = (idx_f[:, i].rearrange("p (c j) -> p c j", c=8) for i in range(3))
            link(nc.vector.tensor_copy(n, idx[:].rearrange("p (c j) -> p c j", c=8)))
            link(nc.vector.scalar_tensor_tensor(wrap, n, 0.0, size, ALU.is_lt, ALU.mult))
            link(nc.vector.tensor_tensor(at, n, wrap, ALU.add))
            link(nc.vector.scalar_tensor_tensor(n, at, 0.0, top, ALU.max, ALU.min))
            nc.vector.tensor_tensor(idx_ok[:].rearrange("p (c j) -> p c j", c=8), n, base, ALU.add
                                    ).then_inc(s_idx_ok, 1)
            dve.wait_ge(s_const, 16 * N_CONST)
            num, wf, bc = (sml[:, k * EMB:(k + 1) * EMB] for k in range(3))
            link(nc.vector.tensor_tensor(wf, wf, bc, ALU.mult))
            link(nc.vector.tensor_tensor(num, num, wf, ALU.mult))
            link(nc.vector.tensor_reduce(beta[:], num, AX.X, ALU.add))
            nc.vector.tensor_scalar(col[:, 0:NT], col[:, 0:NT], 1.0, None, ALU.add).then_inc(s_b1, 1)
            dve.wait_ge(s_uc, 48)
            nc.vector.tensor_tensor(u_c[:, 0], u_c[:, 0], u_prod, ALU.mult).then_inc(s_u, 1)
            nc.vector.tensor_tensor(u_c[:, 1], u_c[:, 1], u_prod, ALU.mult).then_inc(s_u, 1)

            def u_product(t, a):
                dve.wait_ge(s_ur, 16 * (t + 1))
                dve.wait_ge(s_u, 4 * t + 2 * a + 3)
                nc.vector.tensor_tensor(u_prod, u_raw, u_c[:, a], ALU.mult).then_inc(s_u, 1)

            def u_sum(t, a):
                dve.wait_ge(s_u, 4 * t + 2 * a + 4)
                nc.vector.tensor_reduce(U[:, t, a * N_NUM:(a + 1) * N_NUM], u_prod.rearrange("p (j e) -> p j e", e=EMB),
                                        AX.X, ALU.add).then_inc(s_u, 1)

            link(nc.vector.memset(U[:, :, 2 * N_NUM:UW], 0.0))
            nc.vector.tensor_copy(U[:, :, 2 * N_NUM], col[:, WF_X:WF_X + NT]).then_inc(s_u, 1)

            for t in range(U_EARLY):
                for a in range(2):
                    u_product(t, a)
                    u_sum(t, a)

            def bias(ph, t):
                return col[:, bass.ds(BIAS[ph.name] + t, 1)]

            def tile(b, k):
                return X[:, b, bass.ds(k, 1), :].rearrange("p a b -> p (a b)")

            def in_order(ph, k):
                return k if ph.kind != "logit" or k < 12 else k + 6

            def halves(ph, parity):
                n = 2 * EMB if ph.paired == EMB else ph.paired
                pairs[0] += 1
                dve.wait_ge(s_swap, pairs[0])
                nc.vector.tensor_tensor(swap[0:n, :], ps[0:n, 3 * parity + 2, :], swap[0:n, :], ALU.add
                                        ).then_inc(s_sum, 1)

            pairs = [0]

            def take(ph, g, m, parity):
                z = ps[:, 3 * parity + m, :]
                if m == 2 and pair_width(ph, g):
                    z = swap[:]
                    dve.wait_ge(s_sum, pairs[0])
                t = 3 * g + m
                if ph.kind == "first":
                    nc.vector.scalar_tensor_tensor(tile(1, t), z, bias(ph, t), tile(ph.x0, t), ALU.add, ALU.mult
                                                   ).then_inc(s_out_tile, 1)
                elif ph.kind == "rest":
                    nc.vector.tensor_tensor(tmp[:, m % 2], z, tile(1, t), ALU.add).then_inc(s_part, 1)
                elif ph.kind == "logit" and g == 4 and m == 2:
                    nc.vector.scalar_tensor_tensor(tmp[0:UW, m % 2], z[0:UW, :], beta[:, 0:1], F[0:UW, ph.half, :],
                                                   ALU.add, ALU.mult).then_inc(s_part, 1)
                else:
                    k = in_order(ph, t) if ph.kind == "logit" else t
                    nc.vector.scalar_tensor_tensor(tmp[:, m % 2], z, bias(ph, k), tile(ph.x0, k),
                                                   ALU.add, ALU.mult).then_inc(s_part, 1)

            def finish(ph, g, m):
                t = 3 * g + m
                if ph.kind == "first":
                    return
                dve.wait_ge(s_part, t + (ph.part0 + 1))
                if ph.kind == "rest":
                    nc.vector.tensor_tensor(tile(1, t), tmp[:, m % 2], tile(ph.x0, t), ALU.mult
                                            ).then_inc(s_out_tile, 1)
                    return
                if ph.kind == "cross":
                    nc.vector.tensor_tensor(tile(ph.dst[0], t), tmp[:, m % 2], tile(ph.src[0], t), ALU.add
                                            ).then_inc(s_out_tile, 1)
                    return
                dve.wait_ge(s_out_tile, t + (ph.tile0 + OUT0))
                if ph.kind == "relu_logit":
                    nc.vector.scalar_tensor_tensor(acc[:], tile(ph.dst[0], ph.dst[1] + t), wf_h(t), acc[:],
                                                   ALU.mult, ALU.add).then_inc(s_out_tile, 1)
                elif g == 4 and m == 2:
                    nc.vector.tensor_tensor(acc[0:UW, :], tmp[0:UW, m % 2], acc[0:UW, :], ALU.add
                                            ).then_inc(s_out_tile, 1)
                else:
                    nc.vector.scalar_tensor_tensor(acc[:], tmp[:, m % 2], wf_x(in_order(ph, t)), acc[:],
                                                   ALU.mult, ALU.add).then_inc(s_out_tile, 1)

            def wf_h(t):
                return col[:, WF_H + t:WF_H + t + 1]

            def wf_x(t):
                return col[:, WF_X + t:WF_X + t + 1]

            for ph in PLAN:
                buf, base = ph.src

                def dve_group(g, parity, ph=ph, buf=buf, base=base):
                    w, pw = width(ph, g), pair_width(ph, g)
                    if static(g) and g == 0:
                        before = (PLAN[ph.index - 1], len(PLAN[ph.index - 1].widths) - 1) if ph.index else None
                    else:
                        before = (ph, g - 1)
                    if ph.name == "L2" and static(g) and g == 0 and ph.half == 0:
                        dve.wait_ge(s_u, U_DONE - 1)
                        nc.vector.tensor_copy(U[:, :, UW:2 * UW], U[:, :, 0:UW]).then_inc(s_u, 1)
                    if ph.name == "M0" and static(g) and g == 0:
                        if ph.half:
                            dve.wait_ge(s_logit, ph.half)
                        link(nc.vector.memset(acc[:], 0.0))

                    def step(q, b, first):
                        s3 = ph.uses * g + 3 * q + ph.use0
                        tiles = ph.c_tiles if b == "C" else [0, 1, 2]
                        u_here = [(u_tile(ph, g, q - a), a) for a in range(2) if static(q) and
                                  u_tile(ph, g, q - a) is not None]
                        for j, t in enumerate(tiles):
                            dve.wait_ge(s_hi, 2 * ph.uses * g + 6 * q + (2 * ph.use0 + 2 * j + 2))
                            for u_t, a in u_here:
                                if ph.name == "L1" and g == 5 and j == 0:
                                    dve.wait_ge(s_out_tile, ph.tile0 + 15 + OUT0)
                                if j == 0:
                                    u_product(u_t, a)
                                if j == 1:
                                    u_sum(u_t, a)
                            m = taken_tile(before, q, j)
                            if m is not None and before[0].kind not in ("partial", "relu", "relu_logit"):
                                if m == 0:
                                    dve.wait_ge(s_pe, ph.uses * g + (ph.use0 + PE0))
                                if ph.name == "L0b" and static(before[1]) and before[1] == 0 and m == 0:
                                    dve.wait_ge(s_early, NT)
                                take(*before, m, 1 - parity)
                            elif static(q) and (q, j) == (2, 0) and before is not None and pair_width(*before):
                                halves(before[0], 1 - parity)
                            k = slot(ph, g, j)
                            stack = j == 2 and b == "C"
                            rows = slice(64, P) if stack else slice(0, P)
                            if t == "F":
                                src = F[rows, ph.half, :]
                            elif b == "C":
                                src = X[rows, buf, base + t, :]
                            else:
                                src = X[:, buf, bass.ds(3 * q + (base + ph.k0 + t), 1), :].rearrange("p a b -> p (a b)")
                            dst = x_hi if stack else x_lo
                            nc.vector.tensor_tensor(dst[rows, k, :], src, x_hi[rows, k, :], ALU.subtract)
                            ww = 2 * P + pw if pw else w
                            if pw:
                                nc.vector.tensor_tensor(w_hi[:, k, ww:ww + pw], raw[b][:, j, ww:ww + pw],
                                                        w_hi[:, k, 2 * P:ww], ALU.subtract)
                            nc.vector.tensor_tensor(w_lo[:, k, 0:ww], raw[b][:, j, 0:ww], w_hi[:, k, 0:ww],
                                                    ALU.subtract).then_inc(s_lo, 1)
                            if m is not None and before[0].kind not in ("partial", "relu"):
                                finish(*before, m)

                    ab_loop(dve, ph, step, straight=True)
                    if ph.c_tiles:
                        step(2 * ph.n_ab, "C", False)

                groups(dve, ph, dve_group)
            last = PLAN[-1]
            dve.wait_ge(s_pe, last.use0 + 5 * last.uses + PE0)
            for m in range(3):
                if m == 2:
                    halves(last, (last.group0 + 4) % 2)
                take(last, 4, m, (last.group0 + 4) % 2)
                finish(last, 4, m)

        @block.tensor
        def _(pe):
            nc.tensor.sem_inc(s_pe, PE0)
            def prep(h, t):
                n = prep_no[(h, t)]
                if n >= 2:
                    pe.wait_ge(s_x0, n - 1)
                bank = ps[:, 6 + n % 2, :]
                k = gather_no[(h, t)]
                pe.wait_ge(s_gather[k % GS], 128 * (k // GS + 1))
                for c in range(4):
                    mm = nc.tensor.transpose(bank[:, c * P:(c + 1) * P], G[:, k % GS, c, :], ident[:])
                mm.then_inc(s_tp, 1)

            pe.wait_ge(s_fold, 32)
            for c in range(A_CHUNKS):
                pe.wait_ge(s_rows[c % 3], 32 * (c // 3 + 1))
                if c >= 2:
                    pe.wait_ge(s_a, c - 1)
                for i in range(7):
                    k = P if i < 6 else EMB
                    mm = nc.tensor.matmul(ps[:, 3 + c % 2, 0:A_CW], fold_w[0:k, i, :], rows_buf[c % 3][0:k, i, :],
                                          start=(i == 0), stop=(i == 6))
                mm.then_inc(s_a_mm, 1)
                if c in a_preps:
                    prep(0, GATHERED[a_preps[c]])
            def logit(half):
                if half == 0:
                    pe.wait_ge(s_x0, len(prep_list))
                done = [ph for ph in PLAN if ph.half == half][-1]
                pe.wait_ge(s_out_tile, done.tile0 + 15 + OUT0)
                nc.tensor.matmul(ps[0:1, 7 - half, :], ones, acc[:], start=True, stop=True).then_inc(s_logit, 1)

            for ph in PLAN:
                def pe_group(g, parity, ph=ph):
                    mt = out_tiles(ph, g)
                    pw = pair_width(ph, g)
                    if ph.name == "L0a" and g == 1:
                        pe.wait_ge(s_a, A_CHUNKS)
                    if not static(g):
                        pe.wait_ge(s_out_tile, 3 * g + (ph.tile0 - 3 + OUT0))
                    elif before_last(ph, g) is not None:
                        bph, bg = before_last(ph, g)
                        if bph.kind == "partial":
                            pe.wait_ge(s_early, 3 * bg + 3)
                        else:
                            pe.wait_ge(s_out_tile, bph.tile0 + 3 * bg + out_tiles(bph, bg) + OUT0)

                    def step(q, b, first):
                        j_prep = 2 if ph.index == 0 and static(g) and g == 0 and q == 0 else 0
                        if ph.half == 1 and ph.name == "L0" and static(g) and g == 0 and static(q) and q == 3:
                            logit(0)
                        tiles = ph.c_tiles if b == "C" else [0, 1, 2]
                        for j, t in enumerate(tiles):
                            if j == j_prep:
                                for h, x0_tile in preps(ph, g, q, prep_at):
                                    prep(h, x0_tile)
                            pe.wait_ge(s_lo, ph.uses * g + 3 * q + (ph.use0 + j + 1 + LO0))
                            stack = j == 2 and b == "C"
                            last_step = b == "C" or (not ph.c_tiles and q == 2 * ph.n_ab - 1)
                            end = last_step and j == len(tiles) - 1
                            if ph.name == "L0b" and static(g) and g == 0 and b == "C" and j == 0:
                                pe.wait_ge(s_early, NT)
                            k = slot(ph, g, j)
                            for m in range(mt):
                                bank = ps[:, 3 * parity + m, :]
                                cs = slice(m * P, (m + 1) * P)
                                paired = m == 2 and pw
                                mm = nc.tensor.matmul(bank, w_hi[:, k, cs], x_hi[:, k, :], start=(first and j == 0),
                                                      stop=bool(end and stack and paired))
                                if not paired:
                                    mm = nc.tensor.matmul(bank, w_lo[:, k, cs], x_hi[:, k, :], start=False,
                                                          stop=(end and stack))
                                if not stack:
                                    mm = nc.tensor.matmul(bank, (w_lo if paired else w_hi)[:, k, cs], x_lo[:, k, :],
                                                          start=False, stop=end)
                            mm.then_inc(s_pe, 1)

                    ab_loop(pe, ph, step, straight=prep_in(ph, g))
                    if ph.c_tiles:
                        step(2 * ph.n_ab, "C", False)

                groups(pe, ph, pe_group)
            logit(1)


def kernel(**inputs):
    import numpy as np
    import concourse.bacc as bacc
    from concourse.bass_utils import run_bass_kernel_spmd as run

    v = {k.replace("L0_rec_", "").replace("r_", "", 1) if k.startswith("r_") else k.replace("L0_rec_", ""):
         np.asarray(a) for k, a in inputs.items()}
    f4 = np.float32

    def feature_rows():
        cat0 = (2 + N_NUM) * EMB
        cat_r = [np.arange(cat0 + P * k, cat0 + P * (k + 1)) for k in range(13)]
        num_r = [np.arange(P * (k + 1), P * (k + 2)) for k in range(6)]
        tail = np.arange(cat0 - EMB, cat0)
        return cat_r[:12] + num_r + [cat_r[12], np.arange(P), np.concatenate([tail, tail])]

    rows = feature_rows()
    allr = np.concatenate(rows)
    Wc, W0, Wh = v["Wc"], v["W0"], v["Wh"]

    def tiles_of(w, in_tiles, out_cols):
        return [w[r][:, out_cols] for r in in_tiles]

    parts = []

    def put(ph, tiles):
        at = 0
        for g in range(len(ph.widths)):
            w = group_width(ph, g)
            cut = [t[:, at:at + w] for t in tiles]
            at += w
            n = len(cut)
            for q in range(0, n, 3):
                parts.append(np.stack(cut[q:q + 3], axis=1).reshape(-1))

    for ph in [ph for ph in PLAN if ph.half == 1]:
        if ph.name == "L0":
            put(ph, tiles_of(Wc[0], rows[:12] + rows[18:20], allr))
        elif ph.name == "M0":
            put(ph, tiles_of(W0, rows[:12] + rows[18:20], np.arange(MLP)))
        elif ph.name[0] == "H":
            put(ph, [Wh[int(ph.name[1])][P * k:P * (k + 1)] for k in range(8)])
        elif ph.name == "L3":
            put(ph, tiles_of(Wc[3], rows, np.concatenate(rows[:12] + rows[18:20])))
        else:
            put(ph, tiles_of(Wc[int(ph.name[1])], rows, allr))
    stream = np.concatenate(parts)
    assert stream.size == STREAM, (stream.size, STREAM)

    num = np.zeros((7 * P, A_COLS), f4)
    n0 = 2 * EMB
    num[:NUMW, :7 * GW] = Wc[0][n0:n0 + NUMW][:, allr]
    num[:NUMW, 7 * GW:] = W0[n0:n0 + NUMW]
    num_rows = np.ascontiguousarray(num.reshape(7, P, A_CHUNKS, A_CW).transpose(2, 1, 0, 3))
    u_rows = np.ascontiguousarray(Wc[3][allr][:, n0:n0 + NUMW].reshape(NT, P, NUMW))

    idx = np.concatenate([v["categorical_feats"], v["user_input"][:, None], v["item_input"][:, None]], axis=1)
    idx = np.ascontiguousarray(idx.reshape(8, P, NF).transpose(1, 0, 2).reshape(P, 8 * NF))
    size = np.array([VOCAB] * N_CAT + [N_ROWS] * 2, f4)
    base = np.array([VOCAB * j for j in range(N_CAT)] + [0, 0], f4)
    idx_cst = np.ascontiguousarray(np.broadcast_to(np.stack([size, size - 1, base]), (P, 3, NF)))

    fold = np.zeros((P, 7, P), f4)
    for j in range(N_NUM):
        r = slice(EMB * (j % 2), EMB * (j % 2) + EMB)
        for c in (0, 64):
            fold[r, j // 2, c + j] = v["num_W"][j]
            fold[r, j // 2, c + N_NUM] = v["num_b"][j]
    feats = np.zeros((P, BATCH), f4)
    for c in (0, 64):
        feats[c:c + N_NUM] = v["numeric_feats"].T
        feats[c + N_NUM:c + N_FOLD] = 1.0
    feats = feats.reshape(P, HALVES, HB)
    of_row = [2 * i + np.arange(P) // EMB for i in range(6)] + [np.full(P, N_NUM - 1)]
    feats_wide = np.ascontiguousarray(np.stack([v["numeric_feats"].T[j] for j in of_row], axis=1)
                                      .reshape(P, 7, HALVES, HB).transpose(2, 0, 1, 3))

    wf = v["Wf"][:, 0]
    u_cst = np.ascontiguousarray(np.broadcast_to(
        np.stack([v["num_W"].reshape(-1), v["num_b"].reshape(-1), wf[n0:n0 + NUMW]]), (P, 3, NUMW)))

    cols = np.zeros((P, N_COLS), f4)
    for i in range(4):
        cols[:, i * NT:(i + 1) * NT] = v["bc"][i][allr].reshape(NT, P).T
    cols[:, 4 * NT:4 * NT + 8] = v["b0"].reshape(8, P).T
    for i in range(3):
        cols[:, 4 * NT + 8 * (i + 1):4 * NT + 8 * (i + 2)] = v["bh"][i].reshape(8, P).T
    cols[:, WF_H:WF_H + 8] = wf[D:].reshape(8, P).T
    wf_cols = wf[:D][allr].reshape(NT, P).T
    cols[:, WF_X:WF_X + NT] = wf_cols

    for i in range(7):
        e = np.arange(P) % EMB
        cols[:, NUM_COL + i] = v["num_W"][of_row[i], e]
        cols[:, NUM_COL + 7 + i] = v["num_b"][of_row[i], e]
    cols[:, N_COLS - 1] = 1.0

    small = np.zeros((P, 3 * EMB + 1 + P), f4)
    for r, name in ((slice(0, N_NUM), "num_W"), (slice(N_NUM, 2 * N_NUM), "num_b")):
        small[r, 0:EMB] = v[name]
        small[r, EMB:2 * EMB] = wf[n0:n0 + NUMW].reshape(N_NUM, EMB)
        small[r, 2 * EMB:3 * EMB] = v["bc"][3][n0:n0 + NUMW].reshape(N_NUM, EMB)
    small[0, 3 * EMB] = v["bf"][0]
    small[:, 3 * EMB + 1:3 * EMB + 1 + P] = np.eye(P, dtype=f4)

    arrays = {
        "stream": stream, "num_rows": num_rows, "u_rows": u_rows,
        "cat": np.ascontiguousarray(v["cat_tables"].reshape(-1, EMB)),
        "user": np.ascontiguousarray(v["user_emb"]), "item": np.ascontiguousarray(v["item_emb"]),
        "idx_in": idx, "idx_cst": idx_cst, "fold": fold, "feats": feats, "feats_wide": feats_wide, "u_cst": u_cst,
        "cols": cols, "small": small,
    }
    nc = bacc.Bacc("TRN2", target_bir_lowering=False, num_devices=1)
    aps = [nc.dram_tensor(k, a.shape, mybir.dt.from_np(a.dtype), kind="ExternalInput").ap()
           for k, a in arrays.items()]
    o = nc.dram_tensor("logits", (1, BATCH), mybir.dt.float32, kind="ExternalOutput").ap()
    build(nc, *aps, o)
    r = run(nc, [arrays], core_ids=[0])
    return r.results[0]["logits"].reshape(BATCH, 1)
```
